# Optimizing a Trainium2 kernel written in Bass

```python
import numpy as np
import jax
import jax.numpy as jnp

def _softmax(x, axis=-1):
    return jax.nn.softmax(x, axis=axis)

def _gelu(x):
    return jax.nn.gelu(x, approximate=True)

def _silu(x):
    return jax.nn.silu(x)

def _sigmoid(x):
    return jax.nn.sigmoid(x)

def _layernorm(x, axis=-1, eps=1e-05):
    m = jnp.mean(x, axis=axis, keepdims=True)
    v = jnp.var(x, axis=axis, keepdims=True)
    return (x - m) / jnp.sqrt(v + eps)

def _scatter_add(tgt, idx, src, axis=0):
    return tgt.at[idx].add(src)

def _segment_sum(src, seg, n):
    return jax.ops.segment_sum(src, seg, n)
kernel_name = 'mk_seq_preln_d1_jaxref_r8_181ca6'

def setup_inputs(seed: int=0):
    np.random.seed(seed)
    _w = jnp.asarray

    def _L0_attn_setup():
        import jax, jax.numpy as jnp
        import numpy as np
        H = 32
        DN = 128
        DR = 64
        DV = 128
        DQ = DN + DR
        HID = 512
        NEG_INF = -1e+30
        key = jax.random.key(seed)
        k0, k1, k2, k3 = jax.random.split(key, 4)
        B, S = (4, 128)
        hidden_states = jax.random.normal(k0, (B, S, HID), dtype=jnp.float32)
        wq = jax.random.normal(k1, (HID, H * DQ), dtype=jnp.float32) * 0.02
        wkv = jax.random.normal(k2, (HID, H * (DN + DV) + DR), dtype=jnp.float32) * 0.02
        wo = jax.random.normal(k3, (H * DV, HID), dtype=jnp.float32) * 0.02
        return {'hidden_states': hidden_states, 'wq': wq, 'wkv': wkv, 'wo': wo}
    _L0_attn_in = _L0_attn_setup()

    def _L0_ffn_setup():
        import jax, jax.numpy as jnp
        import numpy as np
        import math
        D = 512
        TOKENS = (4, 256)
        P = 0.8

        def conn_dense(kernel, x):
            w = jnp.where(kernel, jnp.asarray(1.0, x.dtype), jnp.asarray(-1.0, x.dtype))
            return x @ w

        def ei_dense(x, kernel, scale, p):
            in_dim = x.shape[-1]
            ne = round(in_dim * p)
            x_exc = x[..., :ne]
            x_inh = x[..., ne:]
            xx = jnp.concatenate([x_exc, -p / (1.0 - p) * x_inh], axis=-1)
            return scale * conn_dense(kernel, xx)
        key = jax.random.key(seed)
        ks = jax.random.split(key, 4)
        x = jax.random.normal(ks[0], (*TOKENS, D), dtype=jnp.float32)
        k0 = jax.random.bernoulli(ks[1], 0.5, (D, D))
        k1 = jax.random.bernoulli(ks[2], 0.5, (D, D))
        k2 = jax.random.bernoulli(ks[3], 0.5, (D, D))
        s = jnp.asarray(1.0 / math.sqrt(D), dtype=jnp.float32)
        return {'x': x, 'k0': k0, 's0': s, 'k1': k1, 's1': s, 'k2': k2, 's2': s}
    _L0_ffn_in = _L0_ffn_setup()
    _d = {'L0_attn_hidden_states': _L0_attn_in['hidden_states'], 'L0_attn_wq': _L0_attn_in['wq'], 'L0_attn_wkv': _L0_attn_in['wkv'], 'L0_attn_wo': _L0_attn_in['wo'], 'L0_ffn_k0': _L0_ffn_in['k0'], 'L0_ffn_s0': _L0_ffn_in['s0'], 'L0_ffn_k1': _L0_ffn_in['k1'], 'L0_ffn_s1': _L0_ffn_in['s1'], 'L0_ffn_k2': _L0_ffn_in['k2'], 'L0_ffn_s2': _L0_ffn_in['s2']}
    _x0 = _d['L0_attn_hidden_states']
    _d['L0_attn_hidden_states'] = jax.random.normal(jax.random.fold_in(jax.random.key(seed), 1), (1, 1024, 512), dtype=_x0.dtype)
    del _x0
    return _d

def reference(L0_attn_hidden_states, L0_attn_wq, L0_attn_wkv, L0_attn_wo, L0_ffn_k0, L0_ffn_s0, L0_ffn_k1, L0_ffn_s1, L0_ffn_k2, L0_ffn_s2):

    def _L0_attn_ref(hidden_states, wq, wkv, wo):
        import jax, jax.numpy as jnp
        import numpy as np
        H = 32
        DN = 128
        DR = 64
        DV = 128
        DQ = DN + DR
        HID = 512
        NEG_INF = -1e+30
        B, S, D = hidden_states.shape
        q = jnp.einsum('bsd,de->bse', hidden_states, wq).reshape(B, S, H, DQ)
        kv = jnp.einsum('bsd,de->bse', hidden_states, wkv)
        k = kv[..., :H * DN].reshape(B, S, H, DN)
        v = kv[..., H * DN:H * (DN + DV)].reshape(B, S, H, DV)
        scale = DQ ** (-0.5)
        scores = jnp.einsum('bqhd,bkhd->bhqk', q[..., :DN], k) * scale
        causal = jnp.tril(jnp.ones((S, S), dtype=bool))
        scores = jnp.where(causal[None, None], scores, NEG_INF)
        probs = jax.nn.softmax(scores, axis=-1)
        attn = jnp.einsum('bhqk,bkhd->bqhd', probs, v).reshape(B, S, H * DV)
        return jnp.einsum('bse,ed->bsd', attn, wo)

    def _L0_ffn_ref(x, k0, s0, k1, s1, k2, s2):
        import jax, jax.numpy as jnp
        import numpy as np
        import math
        D = 512
        TOKENS = (4, 256)
        P = 0.8

        def conn_dense(kernel, x):
            w = jnp.where(kernel, jnp.asarray(1.0, x.dtype), jnp.asarray(-1.0, x.dtype))
            return x @ w

        def ei_dense(x, kernel, scale, p):
            in_dim = x.shape[-1]
            ne = round(in_dim * p)
            x_exc = x[..., :ne]
            x_inh = x[..., ne:]
            xx = jnp.concatenate([x_exc, -p / (1.0 - p) * x_inh], axis=-1)
            return scale * conn_dense(kernel, xx)
        h = s0 * conn_dense(k0, x)
        h = jax.nn.relu(h) * 2.0
        h = ei_dense(h, k1, s1, P)
        h = jax.nn.relu(h) * 2.0
        return ei_dense(h, k2, s2, P)
    x = L0_attn_hidden_states
    x = x + _L0_attn_ref(_layernorm(x, axis=-1), L0_attn_wq, L0_attn_wkv, L0_attn_wo)
    x = x + _L0_ffn_ref(_layernorm(x, axis=-1), L0_ffn_k0, L0_ffn_s0, L0_ffn_k1, L0_ffn_s1, L0_ffn_k2, L0_ffn_s2)
    return x

_drawn_inputs = setup_inputs


def setup_inputs(seed=0):
    import zlib

    import numpy as np

    out = dict(_drawn_inputs(seed))
    spreads = {}
    factors = {'L0_attn_wq': 6.926}
    for name, (base, spread) in spreads.items():
        noise = np.random.default_rng([zlib.crc32(name.encode()), seed]).standard_normal(out[name].shape)
        drawn = base * np.exp(spread * noise) if base else spread * noise
        out[name] = jnp.asarray(drawn.astype(out[name].dtype))
    for name, factor in factors.items():
        out[name] = (out[name] * factor).astype(out[name].dtype)
    return out
```

```python
from contextlib import ExitStack

import concourse.bass as bass
from concourse import mybir

ALU = mybir.AluOpType
ACT = mybir.ActivationFunctionType
AX_X = mybir.AxisListType.X
F32 = mybir.dt.float32
F32R = mybir.dt.float32r
U8 = mybir.dt.uint8

P = 128
CH = 512
DN = 128
GH = 4
HI, LO = 0, 1

SLOT = [("s", 0), ("s", 1), ("pv1", 0), ("o", 0), ("o", 1), ("v", 0), ("t", 0), ("s", 2), ("v", 1),
        ("qk", 0), ("t", 1), ("s", 3), ("v", 2), ("v", 3), ("qk", 1), ("t", 2), ("s", 4), ("v", 4),
        ("o", 2), ("o", 3), ("v", 5), ("t", 3), ("s", 5), ("v", 6), ("qk", 2), ("v", 7), ("pv0", 0),
        ("t", 4), ("s", 6), ("o", 4), ("t", 5), ("s", 7), ("qk", 3), ("t", 6), ("o", 5), ("t", 7),
        ("o", 6), ("o", 7)]
AHEAD = {"qk": 1, "pv1": -1, "o": -1}
CHAINS = ("qk", "v", "pv0", "pv1", "o")


def group_steps(first, last):
    out = []
    for j in range(GH):
        for step, n in SLOT:
            if step == "v" and j != 0:
                continue
            if first and j == 0 and step in ("pv1", "o"):
                continue
            if last and j == GH - 1 and step == "qk":
                continue
            out.append((j, step, n))
    return out


def chain_use(j, step, n):
    if step in ("pv0", "pv1"):
        return "pv", j + AHEAD.get(step, 0), int(step == "pv1")
    return step, j + AHEAD.get(step, 0), n


def chain_banks():
    banks, n = {}, 0
    for j, step, i in group_steps(False, False):
        if step in CHAINS:
            banks[j, step, i] = n % 2
            n += 1
    assert n % 2 == 0
    return banks


BANK = chain_banks()


def chain_before(first, last):
    if first:
        held = {n % 2: ("qk", 0, n) for n in range(4)}
    else:
        held = {}
        for j, step, n in group_steps(False, False):
            if step in CHAINS:
                kind, head, i = chain_use(j, step, n)
                held[BANK[j, step, n]] = (kind, head - GH, i)
    before = {}
    for j, step, n in group_steps(first, last):
        if step in CHAINS:
            b = BANK[j, step, n]
            before[j, step, n] = held[b]
            held[b] = chain_use(j, step, n)
    return before, held


PER_HEAD = {"qk": 4, "v": 2, "pv": 2, "o": 8}


def t_groups(i):
    return i + 1 if i < 4 else 4 + 2 * (i - 3)


def block_at(kt, i):
    return 1 + 8 * kt + i if kt < 4 else 2 + 9 * (7 - kt) + i


def build(nc, hidden, wq, wkv, wo, k0, s0, k1, s1, k2, s2, out):
    _, S, D = hidden.shape
    H = wo.shape[0] // DN
    DQ = wq.shape[1] // H
    SCALE = float(DQ) ** -0.5
    EPS = 1e-5
    NT = S // P
    NC = S // CH
    DC = D // P
    NG = H // GH
    assert (NT, NC, DC, D) == (8, 2, 4, CH) and NG >= 3
    NE = round(D * 0.8)
    INH = -4.0

    x_v = hidden.rearrange("b (t p) d -> p (b t) d", p=P)
    out_v = out.rearrange("b (t p) d -> p (b t) d", p=P)
    wq_v = wq.rearrange("(c p) (h e) -> p c h e", p=P, e=DQ)
    wk_v = wkv[:, 0:H * DN].rearrange("(c p) (h e) -> p c h e", p=P, e=DN)
    wv_v = wkv[:, H * DN:2 * H * DN].rearrange("(c p) (g e) -> p c g e", p=P, e=GH * DN)
    wo_v = wo.rearrange("(h p) d -> p h d", p=P)
    kern_v = [k.rearrange("(c p) n -> p c n", p=P) for k in (k0, k1, k2)]

    with ExitStack() as ctx:
        def sb(name, shape, dt):
            return ctx.enter_context(nc.sbuf_tensor(name, shape, dt))

        def psum(name, shape):
            return ctx.enter_context(nc.psum_tensor(name, shape, F32))

        def sem(name):
            return ctx.enter_context(nc.semaphore(name))

        xT = sb("xT", [P, 2, DC, S], F32R)
        res = sb("res", [P, NT, D], F32)
        v = sb("v", [P, 2, NT, GH * DN], F32R)
        pT = sb("pT", [P, 2, 37, P], F32R)
        qkT = sb("qkT", [P, 2, 2, 2, S], F32R)
        attn = sb("attn", [P, 2, S], F32R)
        probs = sb("probs", [P, 2, S], F32)
        raw = sb("raw", [P, 4, 512], F32)
        wqk = sb("wqk", [P, 2, 2, DC, DN], F32R)
        wvs = sb("wvs", [P, 2, DC, GH * DN], F32R)
        wos = sb("wos", [P, 2, D], F32R)
        ident = sb("ident", [P, P], F32)
        mask = sb("mask", [P, P], F32)
        one = sb("one", [P, 1], F32)
        negmax = sb("negmax", [P, NT], F32)
        rowsum = sb("rowsum", [P, 2, NT], F32)
        rinv = sb("rinv", [P, NT], F32)
        stats = sb("stats", [P, NT, 6], F32)
        mv = sb("mv", [P, NT, 2], F32)
        nrm = sb("nrm", [P, 5, 4], F32)
        slope = sb("slope", [P, DC], F32)
        base = sb("base", [P, DC], F32)
        scl = sb("scl", [P, 3], F32)
        scl2 = sb("scl2", [P, 3], F32)
        xn = probs[:, :, :].rearrange("p a (b d) -> p (a b) d", d=D)
        w_ffn = [wvs[:, 0], wvs[:, 1], wqk[:, :, :, :, :].rearrange("p a b c e -> p (a b c e)")
                 .rearrange("p (c n) -> p c n", n=D)]
        h1T = qkT[:, :, :, :, :].rearrange("p a b c s -> p (a b c s)") \
            .rearrange("p (w c s) -> p w c s", w=2, c=DC)
        h2T = v[:, :, :, :].rearrange("p a t e -> p (a t e)") \
            .rearrange("p (w c s) -> p w c s", w=2, c=DC)
        relu = probs[:, :, :].rearrange("p a (b s) -> p (a b) s", s=CH)

        psS = psum("psS", [P, 2, 1024])
        psT = psum("psT", [P, 2, CH])
        psC = psum("psC", [P, 2, CH])
        psF = psS[:, :, :].rearrange("p a (b n) -> p (a b) n", n=CH)

        x_in = [sem(f"x_in{t}") for t in range(NT)]
        scl_in = sem("scl_in")
        loaded = {k: sem(f"loaded_{k}") for k in ("q", "k", "o", "v")}
        whi = {k: sem(f"whi_{k}") for k in ("q", "k", "o", "v")}
        wready = {k: sem(f"wready_{k}") for k in ("q", "k", "o", "v")}
        kern_in = sem("kern_in")
        w_ffn_ready = sem("w_ffn_ready")
        const_set = sem("const_set")
        const_ready = sem("const_ready")
        zero_ready = sem("zero_ready")
        done = {k: sem(f"{k}_done") for k in ("qk", "v", "s", "t", "pv", "o")}
        hi_done = {k: sem(f"{k}_hi") for k in ("qk", "v", "t", "pv")}
        lo_done = {k: sem(f"{k}_lo") for k in ("qk", "v", "t", "pv")}
        exp_done = sem("exp_done")
        masked = sem("masked")
        max_done = sem("max_done")
        rinv_done = sem("rinv_done")
        added = sem("added")
        evacuated = {"qk": lo_done["qk"], "v": lo_done["v"], "pv": lo_done["pv"], "o": added}
        ve_done = sem("ve_done")
        root_done = sem("root_done")
        xn_done = sem("xn_done")
        xt_done = sem("xt_done")
        xt_hi = sem("xt_hi")
        xt_lo = sem("xt_lo")
        chain_dve = sem("chain_dve")
        scl_ready = sem("scl_ready")
        f_done = sem("f_done")
        relu_done = sem("relu_done")
        h_hi = sem("h_hi")
        h_lo = sem("h_lo")
        y_done = sem("y_done")
        stored = sem("stored")
        block = ctx.enter_context(nc.Block())

        def count(g, j, per, n):
            return g * (GH * per) + (per * j + n)

        def wait(eng, s, value):
            if not isinstance(value, int) or value > 0:
                eng.wait_ge(s, value)

        def groups(eng, body):
            body(0, True, False)
            with eng.Fori(1, NG - 1) as g:
                body(g, False, False)
            body(NG - 1, False, True)

        @block.sync
        def _(sp):
            def load_head(kind, g, j):
                wait(sp, wready[kind], count(g, j, 1, 0))
                h = g * GH + j
                if kind == "o":
                    sp.dma_start(raw[:, 2, :], wo_v[:, bass.ds(h, 1), :].rearrange("p a d -> p (a d)")) \
                        .then_inc(loaded[kind], 16)
                else:
                    n, src = (0, wq_v) if kind == "q" else (1, wk_v)
                    sp.dma_start(raw[:, n, :].rearrange("p (c e) -> p c e", e=DN),
                                 src[:, :, bass.ds(h, 1), 0:DN].rearrange("p c a e -> p c (a e)")) \
                        .then_inc(loaded[kind], 16)

            def load_values(g, c):
                wait(sp, wready["v"], count(g, 0, 1, c))
                sp.dma_start(raw[:, 3, :], wv_v[:, c, bass.ds(g, 1), :].rearrange("p a e -> p (a e)")) \
                    .then_inc(loaded["v"], 16)

            for t in range(4):
                sp.dma_start(res[:, t, :], x_v[:, t, :]).then_inc(x_in[t], 16)
            load_head("q", 0, 0)
            load_head("k", 0, 0)
            for t in range(4, NT):
                sp.dma_start(res[:, t, :], x_v[:, t, :]).then_inc(x_in[t], 16)
            for n, s in enumerate((s0, s1, s2)):
                sp.dma_start(scl[:, n:n + 1], s.partition_broadcast(P)).then_inc(scl_in, 16)
            for c in range(DC):
                load_values(0, c)
            load_head("q", 0, 1)
            load_head("k", 0, 1)

            def body(g, first, last):
                for j in range(GH):
                    if not last or j < GH - 2:
                        load_head("q", g, j + 2)
                        load_head("k", g, j + 2)
                    if not last:
                        load_values(g + 1, j)
                    elif j < 3:
                        if j == 0:
                            sp.wait_ge(wready["v"], NG * DC)
                        else:
                            sp.wait_ge(w_ffn_ready, 4 * j)
                        sp.dma_start(raw[:, 3, :].bitcast(U8).rearrange("p (c n) -> p c n", n=D),
                                     kern_v[j]).then_inc(kern_in, 16)
                    load_head("o", g, j)

            groups(sp, body)
            for t in range(NT):
                sp.wait_ge(y_done, t + 1)
                sp.dma_start(out_v[:, t, :], res[:, t, :]).then_inc(stored, 16)
            sp.wait_ge(stored, 16 * NT)

        @block.gpsimd
        def _(pool):
            def cut(kind, n, count_ready, hi, lo):
                nc.gpsimd.tensor_tensor(hi, raw[:, n, :], one[:, :].to_broadcast([P, 512]), ALU.mult).then_inc(whi[kind], 1)
                pool.wait_ge(whi[kind], count_ready)
                nc.gpsimd.tensor_tensor(lo, raw[:, n, :], hi.bitcast(F32), ALU.subtract) \
                    .then_inc(wready[kind], 1)

            def cut_head(kind, g, j):
                pool.wait_ge(loaded[kind], count(g, j, 16, 16))
                if kind == "o":
                    wait(pool, done["o"], count(g, j, 8, 0))
                    cut("o", 2, count(g, j, 1, 1), wos[:, HI, :], wos[:, LO, :])
                else:
                    n = int(kind == "k")
                    wait(pool, done["qk"], count(g, j, 4, 2 * n - 2))
                    w = wqk[:, n].rearrange("p w c e -> p w (c e)")
                    cut(kind, n, count(g, j, 1, 1), w[:, HI], w[:, LO])

            def cut_values(g, c):
                pool.wait_ge(loaded["v"], count(g, 0, 16, 16 * c + 16))
                if c == 0:
                    wait(pool, done["v"], count(g, 0, 2, 0))
                cut("v", 3, count(g, 0, 1, c + 1), wvs[:, HI, c, :], wvs[:, LO, c, :])

            nc.gpsimd.memset(ident[:, :], 0.0).then_inc(const_set, 1)
            nc.gpsimd.memset(mask[:, :], 0.0).then_inc(const_set, 1)
            nc.gpsimd.memset(slope[:, :], 2.0).then_inc(const_set, 1)
            nc.gpsimd.memset(base[:, :], -1.0).then_inc(const_set, 1)
            nc.gpsimd.memset(one[:, :], 1.0).then_inc(const_set, 1)
            pool.wait_ge(const_set, 5)
            nc.gpsimd.affine_select(out=ident[:, :], in_=ident[:, :], compare_op=ALU.not_equal, fill=1.0,
                                    base=0, pattern=[[-1, P]], channel_multiplier=1).then_inc(const_ready, 1)
            nc.gpsimd.affine_select(out=mask[:, :], in_=mask[:, :], compare_op=ALU.is_ge, fill=-1e30,
                                    base=0, pattern=[[-1, P]], channel_multiplier=1).then_inc(const_ready, 1)
            for col, value in ((slope, 2.0), (base, -1.0)):
                part = col[:, NE // P:NE // P + 1]
                nc.gpsimd.affine_select(out=part, in_=part, compare_op=ALU.is_ge, fill=value * INH,
                                        base=NE % P - 1, pattern=[[0, 1]], channel_multiplier=-1) \
                    .then_inc(const_ready, 1)
            cut_head("q", 0, 0)
            cut_head("k", 0, 0)
            for c in range(DC):
                cut_values(0, c)
            cut_head("q", 0, 1)
            cut_head("k", 0, 1)

            def ffn_weights(n):
                pool.wait_ge(kern_in, 16 * n + 16)
                if n == 0:
                    pool.wait_ge(done["v"], NG * NT)
                    pool.wait_ge(const_ready, 4)
                if n == 2:
                    pool.wait_ge(done["qk"], 4 * H)
                bits = raw[:, 3, :].bitcast(U8).rearrange("p (c n) -> p c n", n=D)
                for c in range(DC):
                    a, b = (2.0, -1.0) if n == 0 else (slope[:, c:c + 1], base[:, c:c + 1])
                    nc.gpsimd.tensor_scalar(w_ffn[n][:, c, :], bits[:, c, :], a, b, ALU.mult, ALU.add) \
                        .then_inc(w_ffn_ready, 1)

            def body(g, first, last):
                for j in range(GH):
                    if not last or j < GH - 2:
                        cut_head("q", g, j + 2)
                        cut_head("k", g, j + 2)
                    if not last:
                        cut_values(g + 1, j)
                    elif j < 2:
                        ffn_weights(j)
                    elif j == 3:
                        ffn_weights(2)
                    cut_head("o", g, j)

            groups(pool, body)

        @block.scalar
        def _(act):
            def norm_root(b):
                act.wait_ge(ve_done, b + 1)
                nc.scalar.activation(nrm[:, 1, :], nrm[:, 0, :], ACT.Sqrt).then_inc(root_done, 1)

            def norm_hi(n):
                t = n % NT
                act.wait_ge(xt_done, n + 1)
                nc.scalar.activation(xT[:, HI, :, t * P:(t + 1) * P],
                                     psT[:, t % 2, :].rearrange("p (c s) -> p c s", s=P), ACT.Copy) \
                    .then_inc(xt_hi, 1)

            for b in range(NC):
                norm_root(b)
                for t in range(4 * b, 4 * b + 4):
                    norm_hi(t)

            def qk_hi(g, j, n, bank):
                side, c = n // 2, n % 2
                act.wait_ge(done["qk"], count(g, j, 4, n + 1))
                nc.scalar.activation(qkT[:, side, j % 2, HI, c * CH:(c + 1) * CH], psC[:, bank, :], ACT.Copy,
                                     scale=SCALE if side == 0 else 1.0).then_inc(hi_done["qk"], 1)

            for n in range(4):
                qk_hi(0, 0, n, n % 2)

            def body(g, first, last):
                for j, step, n in group_steps(first, last):
                    bank = BANK.get((j, step, n))
                    if step == "s":
                        width = (n + 1) * P
                        off = P if n == 4 else 0
                        act.wait_ge(max_done, count(g, j, 8, n + 1))
                        if n >= 2:
                            act.wait_ge(done["t"], count(g, j, 12, t_groups(n - 2)))
                        else:
                            wait(act, done["t"], count(g, j - 1, 12, t_groups(n + 6)))
                        nc.scalar.activation(probs[:, n % 2, 0:width], psS[:, n % 2, off:off + width], ACT.Exp,
                                             bias=negmax[:, n:n + 1], accum_out=rowsum[:, j % 2, n:n + 1]) \
                            .then_inc(exp_done, 1)
                    elif step == "t":
                        for k in range(1 if n < 4 else 2):
                            m = (t_groups(n - 1) if n else 0) + k
                            dst, width = pT_group(n, k)
                            act.wait_ge(done["t"], count(g, j, 12, m + 1))
                            nc.scalar.activation(pT[:, HI, dst, :],
                                                 psT[:, m % 2, 0:width].rearrange("p (b s) -> p b s", s=P),
                                                 ACT.Copy).then_inc(hi_done["t"], 1)
                    elif step == "qk":
                        qk_hi(g, j + 1, n, bank)
                    elif step == "v":
                        act.wait_ge(done["v"], count(g, 0, 2, n + 1))
                        nc.scalar.activation(v[:, HI, n, :], psC[:, bank, :], ACT.Copy) \
                            .then_inc(hi_done["v"], 1)
                    elif step in ("pv0", "pv1"):
                        pv_hi(g, j + AHEAD.get(step, 0), int(step == "pv1"), bank)

            def pv_hi(g, j, c, bank):
                act.wait_ge(done["pv"], count(g, j, 2, c + 1))
                wait(act, done["o"], count(g, j, 8, 4 * c - 4))
                nc.scalar.activation(attn[:, HI, c * CH:(c + 1) * CH], psC[:, bank, :], ACT.Copy) \
                    .then_inc(hi_done["pv"], 1)

            groups(act, body)
            pv_hi(NG - 1, GH - 1, 1, END["pv"])

            for b in range(NC):
                norm_root(NC + b)
                for t in range(4 * b, 4 * b + 4):
                    norm_hi(NT + t)

            act.wait_ge(scl_ready, 1)
            for layer, hT in enumerate((h1T, h2T)):
                for n in range(NT):
                    c, do = n // 4, n % 4
                    m = NT * layer + n
                    act.wait_ge(f_done, m + 1)
                    if m >= 4:
                        act.wait_ge(h_lo, m - 3)
                    nc.scalar.activation(relu[:, n % 4, :], psF[:, n % 4, :], ACT.Relu,
                                         scale=scl2[:, layer:layer + 1]).then_inc(relu_done, 1)
                    nc.scalar.activation(hT[:, HI, do, c * CH:(c + 1) * CH], psF[:, n % 4, :], ACT.Relu,
                                         scale=scl2[:, layer:layer + 1]).then_inc(h_hi, 1)

        @block.vector
        def _(dve):
            links = [0]

            def link(ins):
                links[0] += 1
                ins.then_inc(chain_dve, 1)
                dve.wait_ge(chain_dve, links[0])

            def norm_batch(b, round_):
                for t in range(4 * b, 4 * b + 4):
                    if round_ == 0:
                        dve.wait_ge(x_in[t], 16)
                    else:
                        dve.wait_ge(added, NT * (H - 1) + t + 1)
                    link(nc.vector.bn_stats(stats[:, t, :], res[:, t, :]))
                    link(nc.vector.bn_aggr(mv[:, t, :], stats[:, t, :]))
                ve, root, inv, a, bb = (nrm[:, k, :] for k in range(5))
                nc.vector.tensor_scalar_add(ve, mv[:, 4 * b:4 * b + 4, 1], EPS).then_inc(ve_done, 1)
                dve.wait_ge(root_done, NC * round_ + b + 1)
                link(nc.vector.reciprocal(inv, root))
                link(nc.vector.tensor_tensor(a, inv, inv, ALU.mult))
                link(nc.vector.tensor_tensor(bb, a, ve, ALU.mult))
                link(nc.vector.tensor_scalar(a, bb, -0.5, 1.5, ALU.mult, ALU.add))
                link(nc.vector.tensor_tensor(bb, inv, a, ALU.mult))
                for t in range(4 * b, 4 * b + 4):
                    n = NT * round_ + t
                    if t >= 4:
                        dve.wait_ge(xt_done, n - 3)
                    nc.vector.tensor_scalar(xn[:, t % 4, :], res[:, t, :], mv[:, t, 0:1], bb[:, t % 4:t % 4 + 1],
                                            ALU.subtract, ALU.mult).then_inc(xn_done, 1)
                for t in range(4 * b, 4 * b + 4):
                    n = NT * round_ + t
                    dve.wait_ge(xt_hi, n + 1)
                    nc.vector.tensor_tensor(xT[:, LO, :, t * P:(t + 1) * P],
                                            psT[:, t % 2, :].rearrange("p (c s) -> p c s", s=P),
                                            xT[:, HI, :, t * P:(t + 1) * P].bitcast(F32), ALU.subtract) \
                        .then_inc(xt_lo, 1)

            nc.vector.memset(pT[:, :, 0, :].bitcast(F32), 0.0).then_inc(zero_ready, 1)
            for b in range(NC):
                norm_batch(b, 0)

            def qk_lo(g, j, n, bank):
                side, c = n // 2, n % 2
                hi, lo = (qkT[:, side, j % 2, w, c * CH:(c + 1) * CH] for w in (HI, LO))
                dve.wait_ge(hi_done["qk"], count(g, j, 4, n + 1))
                nc.vector.scalar_tensor_tensor(lo, psC[:, bank, :], SCALE if side == 0 else 1.0, hi.bitcast(F32),
                                               ALU.mult, ALU.subtract).then_inc(lo_done["qk"], 1)

            def pv_lo(g, j, c, bank):
                hi, lo = (attn[:, w, c * CH:(c + 1) * CH] for w in (HI, LO))
                dve.wait_ge(hi_done["pv"], count(g, j, 2, c + 1))
                nc.vector.tensor_tensor(lo, psC[:, bank, :], hi.bitcast(F32), ALU.subtract) \
                    .then_inc(lo_done["pv"], 1)

            def invert_sums(g, j):
                dve.wait_ge(exp_done, count(g, j, 8, 8))
                wait(dve, added, count(g, j, 8, 0))
                nc.vector.reciprocal(rinv[:, :], rowsum[:, j % 2, :]).then_inc(rinv_done, 1)

            def add_output(g, j, t, bank):
                if t == 0:
                    dve.wait_ge(rinv_done, count(g, j, 1, 1))
                dve.wait_ge(done["o"], count(g, j, 8, t + 1))
                wait(dve, added, count(g, j, 8, t - 7))
                nc.vector.scalar_tensor_tensor(res[:, t, :], psC[:, bank, :], rinv[:, t:t + 1], res[:, t, :],
                                               ALU.mult, ALU.add).then_inc(added, 1)

            for n in range(4):
                qk_lo(0, 0, n, n % 2)

            def body(g, first, last):
                if first:
                    dve.wait_ge(const_ready, 2)
                for j, step, n in group_steps(first, last):
                    bank = BANK.get((j, step, n))
                    if step == "s":
                        width = (n + 1) * P
                        off = P if n == 4 else 0
                        diag = psS[:, n % 2, off + width - P:off + width]
                        dve.wait_ge(done["s"], count(g, j, 8, n + 1))
                        nc.vector.tensor_tensor(diag, diag, mask[:, :], ALU.add).then_inc(masked, 1)
                        dve.wait_ge(masked, count(g, j, 8, n + 1))
                        nc.vector.tensor_reduce(negmax[:, n:n + 1], psS[:, n % 2, off:off + width], AX_X, ALU.max,
                                                negate=True).then_inc(max_done, 1)
                    elif step == "t":
                        for k in range(1 if n < 4 else 2):
                            m = (t_groups(n - 1) if n else 0) + k
                            dst, width = pT_group(n, k)
                            dve.wait_ge(hi_done["t"], count(g, j, 12, m + 1))
                            nc.vector.tensor_tensor(pT[:, LO, dst, :],
                                                    psT[:, m % 2, 0:width].rearrange("p (b s) -> p b s", s=P),
                                                    pT[:, HI, dst, :].bitcast(F32), ALU.subtract) \
                                .then_inc(lo_done["t"], 1)
                    elif step == "qk":
                        qk_lo(g, j + 1, n, bank)
                    elif step == "v":
                        dve.wait_ge(hi_done["v"], count(g, 0, 2, n + 1))
                        nc.vector.tensor_tensor(v[:, LO, n, :], psC[:, bank, :], v[:, HI, n, :].bitcast(F32),
                                                ALU.subtract).then_inc(lo_done["v"], 1)
                    elif step == "pv0":
                        pv_lo(g, j, 0, bank)
                    elif step == "pv1":
                        pv_lo(g, j - 1, 1, bank)
                        invert_sums(g, j - 1)
                    elif step == "o":
                        add_output(g, j - 1, n, bank)

            groups(dve, body)
            pv_lo(NG - 1, GH - 1, 1, END["pv"])
            invert_sums(NG - 1, GH - 1)
            for t in range(NT):
                add_output(NG - 1, GH - 1, t, END["o", t])

            dve.wait_ge(scl_in, 48)
            nc.vector.tensor_scalar_mul(scl2[:, :], scl[:, :], 2.0).then_inc(scl_ready, 1)
            for b in range(NC):
                norm_batch(b, 1)
            for layer, hT in enumerate((h1T, h2T)):
                for n in range(NT):
                    c, do = n // 4, n % 4
                    m = NT * layer + n
                    dve.wait_ge(relu_done, m + 1)
                    dve.wait_ge(h_hi, m + 1)
                    nc.vector.tensor_tensor(hT[:, LO, do, c * CH:(c + 1) * CH], relu[:, n % 4, :],
                                            hT[:, HI, do, c * CH:(c + 1) * CH].bitcast(F32), ALU.subtract) \
                        .then_inc(h_lo, 1)
            for t in range(NT):
                dve.wait_ge(f_done, 2 * NT + t + 1)
                nc.vector.scalar_tensor_tensor(res[:, t, :], psF[:, t % 4, :], scl[:, 2:3], res[:, t, :],
                                               ALU.mult, ALU.add).then_inc(y_done, 1)

        @block.tensor
        def _(pe):
            def chain(out_ap, terms):
                for k, (w, x) in enumerate(terms):
                    last = nc.tensor.matmul(out_ap, w, x, start=(k == 0), stop=(k == len(terms) - 1))
                return last

            def halves(w, x):
                return [(w(HI), x(HI)), (w(HI), x(LO)), (w(LO), x(HI))]

            def norm_transpose(n):
                t = n % NT
                pe.wait_ge(xn_done, n + 1)
                if t >= 2:
                    pe.wait_ge(xt_lo, n - 1)
                for c in range(DC):
                    last = nc.tensor.transpose(psT[:, t % 2, c * P:(c + 1) * P],
                                               xn[:, t % 4, c * P:(c + 1) * P], ident[:, :])
                last.then_inc(xt_done, 1)

            def project_qk(g, j, n, bank):
                side, c = n // 2, n % 2
                if c == 0:
                    pe.wait_ge(wready["qk"[side]], count(g, j, 1, 1))
                terms = []
                for d in range(DC):
                    terms += halves(lambda w: wqk[:, side, w, d, :], lambda w: xT[:, w, d, c * CH:(c + 1) * CH])
                chain(psC[:, bank, :], terms).then_inc(done["qk"], 1)

            pe.wait_ge(const_ready, 1)
            for t in range(NT):
                norm_transpose(t)
            for n in range(4):
                pe.wait_ge(xt_lo, 4 if n % 2 == 0 else NT)
                if n >= 2:
                    pe.wait_ge(lo_done["qk"], n - 1)
                project_qk(0, 0, n, n % 2)

            def values(g, j, c, bank):
                pe.wait_ge(lo_done["t"], count(g, j, 12, t_groups(4 * c + 3)))
                if c == 0 and j == 0:
                    pe.wait_ge(lo_done["v"], count(g, 0, 2, NT))
                keys = 4 * c + 4
                for kt in range(keys):
                    i = max(4 * c, kt)
                    at, n = block_at(kt, i), 4 * c + 4 - i
                    cols = slice(0, at + 1, at) if n == 1 else slice(at, at + n)
                    o = psC[:, bank, (4 - max(n, 2)) * P:]
                    if n == 1:
                        o = o.rearrange("p (b s) -> p b s", s=P)
                    terms = halves(lambda w: v[:, w, kt, j % GH * DN:(j % GH + 1) * DN],
                                   lambda w: pT[:, w, cols, :] if n == 1 else
                                   pT[:, w, cols, :].rearrange("p b s -> p (b s)"))
                    for k, (a, b) in enumerate(terms):
                        last = nc.tensor.matmul(o, a, b, start=(kt == 0 and k == 0),
                                                stop=(kt == keys - 1 and k == 2))
                last.then_inc(done["pv"], 1)

            def project_out(g, j, t, bank):
                if t == 0:
                    pe.wait_ge(wready["o"], count(g, j, 1, 1))
                if t % 4 == 0:
                    pe.wait_ge(lo_done["pv"], count(g, j, 2, t // 4 + 1))
                chain(psC[:, bank, :], halves(lambda w: attn[:, w, t * P:(t + 1) * P], lambda w: wos[:, w, :])) \
                    .then_inc(done["o"], 1)

            def body(g, first, last_group):
                before, _ = chain_before(first, last_group)
                if first:
                    pe.wait_ge(zero_ready, 1)
                for j, step, n in group_steps(first, last_group):
                    bank = BANK.get((j, step, n))
                    if step in CHAINS:
                        kind, head, k = before[j, step, n]
                        pe.wait_ge(evacuated[kind], count(g, head, PER_HEAD[kind], k + 1))
                    if step == "s":
                        if n == 0:
                            pe.wait_ge(lo_done["qk"], count(g, j, 4, 4))
                        wait(pe, exp_done, count(g, j, 8, n - 1))
                        q = lambda w: qkT[:, 0, j % 2, w, n * P:(n + 1) * P]
                        off = P if n == 4 else 0
                        first_cols = 3 * P if n == 4 else min(4, max(2, n + 1)) * P
                        spans = [(0, first_cols)]
                        if n >= 4:
                            spans.append((first_cols, (n + 1) * P))
                        for a, b in spans:
                            last = chain(psS[:, n % 2, off + a:off + b],
                                         halves(q, lambda w: qkT[:, 1, j % 2, w, a:b]))
                        last.then_inc(done["s"], 1)
                    elif step == "t":
                        pe.wait_ge(exp_done, count(g, j, 8, n + 1))
                        for k in range(1 if n < 4 else 2):
                            m = (t_groups(n - 1) if n else 0) + k
                            wait(pe, lo_done["t"], count(g, j, 12, m - 1))
                            tiles = range(min(n, 3) + 1) if k == 0 else range(n, 3, -1)
                            for u, kt in enumerate(tiles):
                                last = nc.tensor.transpose(psT[:, m % 2, u * P:(u + 1) * P],
                                                           probs[:, n % 2, kt * P:(kt + 1) * P], ident[:, :])
                            last.then_inc(done["t"], 1)
                    elif step == "qk":
                        project_qk(g, j + 1, n, bank)
                    elif step == "v":
                        if n == 0:
                            pe.wait_ge(wready["v"], count(g, 0, 1, DC))
                        terms = []
                        for d in range(DC):
                            terms += halves(lambda w: xT[:, w, d, n * P:(n + 1) * P], lambda w: wvs[:, w, d, :])
                        chain(psC[:, bank, :], terms).then_inc(done["v"], 1)
                    elif step == "pv0":
                        values(g, j, 0, bank)
                    elif step == "pv1":
                        values(g, j - 1, 1, bank)
                    elif step == "o":
                        project_out(g, j - 1, n, bank)

            groups(pe, body)

            for use in [("pv", 1)] + [("o", t) for t in range(NT)]:
                kind, n = use
                bank = END["pv"] if kind == "pv" else END["o", n]
                k_before, h_before, n_before = END_BEFORE[use]
                pe.wait_ge(evacuated[k_before], count(NG - 1, h_before, PER_HEAD[k_before], n_before + 1))
                if kind == "pv":
                    values(NG - 1, GH - 1, 1, bank)
                else:
                    project_out(NG - 1, GH - 1, n, bank)

            for t in range(NT):
                norm_transpose(NT + t)
            for layer, src in enumerate((xT, h1T)):
                for n in range(NT):
                    c, do = n // 4, n % 4
                    m = NT * layer + n
                    if do == 0:
                        if layer == 0:
                            pe.wait_ge(xt_lo, NT + 4 * c + 4)
                        else:
                            pe.wait_ge(h_lo, 4 * c + 4)
                    if n == 0:
                        pe.wait_ge(w_ffn_ready, DC * (layer + 1))
                    if m >= 4:
                        pe.wait_ge(h_lo, m - 3)
                    terms = [(w_ffn[layer][:, d, do * P:(do + 1) * P], src[:, w, d, c * CH:(c + 1) * CH])
                             for d in range(DC) for w in (HI, LO)]
                    chain(psF[:, n % 4, :], terms).then_inc(f_done, 1)
            for t in range(NT):
                if t == 0:
                    pe.wait_ge(w_ffn_ready, 3 * DC)
                if t < 4:
                    pe.wait_ge(h_lo, 2 * NT - 3 + t)
                    pe.wait_ge(h_lo, NT + 4)
                else:
                    pe.wait_ge(y_done, t - 3)
                if t == 4:
                    pe.wait_ge(h_lo, 2 * NT)
                terms = [(h2T[:, w, d, t * P:(t + 1) * P], w_ffn[2][:, d, :]) for d in range(DC) for w in (HI, LO)]
                chain(psF[:, t % 4, :], terms).then_inc(f_done, 1)


def pT_group(n, k):
    if k == 0:
        m = min(n, 3) + 1
        return slice(block_at(0, n), block_at(0, n) + 8 * (m - 1) + 1, 8), m * P
    m = n - 3
    return slice(block_at(n, n), block_at(n, n) + 9 * (m - 1) + 1, 9), m * P


def chain_end():
    _, held = chain_before(False, True)
    banks, before = {"pv": 0}, {("pv", 1): held[0]}
    held[0] = ("pv", GH - 1, 1)
    for t in range(8):
        b = (t + 1) % 2
        banks["o", t] = b
        before["o", t] = held[b]
        held[b] = ("o", GH - 1, t)
    return banks, before


END, END_BEFORE = chain_end()

_INS = ["L0_attn_hidden_states", "L0_attn_wq", "L0_attn_wkv", "L0_attn_wo", "L0_ffn_k0", "L0_ffn_s0",
        "L0_ffn_k1", "L0_ffn_s1", "L0_ffn_k2", "L0_ffn_s2"]


def kernel(**inputs):
    import numpy as _np
    import concourse.bacc as _bacc
    from concourse import mybir as _mybir
    from concourse.bass_utils import run_bass_kernel_spmd as _run

    nc = _bacc.Bacc("TRN2", target_bir_lowering=False, num_devices=1)
    arrays, args = {}, []
    for name in _INS:
        a = _np.ascontiguousarray(inputs[name])
        arrays[f"in_{name}"] = a
        args.append(nc.dram_tensor(f"in_{name}", a.shape, _mybir.dt.from_np(a.dtype), kind="ExternalInput").ap())
    shape = inputs["L0_attn_hidden_states"].shape
    args.append(nc.dram_tensor("out", shape, _mybir.dt.float32, kind="ExternalOutput").ap())
    build(nc, *args)
    r = _run(nc, [arrays], core_ids=[0])
    return r.results[0]["out"]
```

```python
from contextlib import ExitStack

import concourse.bass as bass
from concourse import mybir

ALU = mybir.AluOpType
ACT = mybir.ActivationFunctionType
AX_X = mybir.AxisListType.X
F32 = mybir.dt.float32
F32R = mybir.dt.float32r
F16 = mybir.dt.float16
U8 = mybir.dt.uint8

P = 128
CH = 512
DN = 128
GH = 2
HI, LO = 0, 1

TENSOR_ORDER = """
    s0@0 qk0@1 s1@0 qk1@1 s2@0 qk2@1 o0@-1 qk3@1 s3@0 s4@0 pv1@-1 s5@0 o1@-1 v0@0 s6@0 o2@-1 v1@0
    v2@0 v3@0 s7@0 qk0@2 o3@-1 v4@0 s0@1 qk1@2 s1@1 o4@-1 v5@0 v6@0 s2@1 qk2@2 v7@0 o5@-1 s3@1 s4@1
    pv0@0 o6@-1 s5@1 o7@-1 pv1@0 o0@0 s6@1 s7@1 o1@0 o2@0 o3@0 o4@0 o5@0 qk3@2 o6@0 pv0@1 o7@0"""
SCALAR_ORDER = """
    pv0@-1 h7@-1 c5@-1 e0@0 qk0@1 qk1@1 e1@0 h0@0 c6@-1 h1@0 e2@0 c7@-1 qk2@1 h2@0 e3@0 qk3@1 h3@0
    e4@0 c0@0 pv1@-1 c1@0 e5@0 h4@0 v0@0 c2@0 v1@0 h5@0 v2@0 c3@0 e6@0 v3@0 h6@0 e7@0 qk0@2 h7@0
    v4@0 c4@0 e0@1 c5@0 h0@1 qk1@2 c6@0 e1@1 v5@0 h1@1 v6@0 e2@1 qk2@2 v7@0 c7@0 h2@1 e3@1 c0@1
    pv0@0 h3@1 e4@1 c1@1 h4@1 e5@1 pv1@0 c2@1 c3@1 h5@1 c4@1 qk3@2 e6@1 h6@1 e7@1"""
VECTOR_ORDER = """
    m0@0 pv0@-1 l7@-1 m1@0 qk0@1 m2@0 l0@0 l1@0 qk1@1 m3@0 qk2@1 m4@0 l2@0 o0@-1 qk3@1 l3@0 m5@0
    o1@-1 pv1@-1 m6@0 v0@0 l4@0 v1@0 l5@0 o2@-1 m7@0 v2@0 l6@0 v3@0 m0@1 qk0@2 v4@0 o3@-1 l7@0 m1@1
    qk1@2 m2@1 o4@-1 v5@0 l0@1 v6@0 l1@1 v7@0 qk2@2 m3@1 m4@1 o5@-1 l2@1 m5@1 l3@1 o6@-1 o7@-1 pv0@0
    l4@1 o0@0 pv1@0 m6@1 o1@0 o2@0 o3@0 o4@0 l5@1 m7@1 o5@0 qk3@2 o6@0 o7@0 l6@1"""
CHAINS = ("qk", "v", "pv", "o")
NB = 4
PER_HEAD = {"qk": 4, "v": 8 // GH, "pv": 2, "o": 8}


def parse(order):
    out = []
    for word in order.split():
        name, head = word.split("@")
        out.append((name[:-1], int(head), int(name[-1])))
    return out


def group_steps(order, first, last):
    return [x for x in parse(order) if not (first and x[1] < 0) and not (last and x[1] >= GH)]


def tail_steps(order):
    return [(step, h + GH, n) for step, h, n in parse(order) if h < 0]


def chain_banks():
    uses = [use for use in parse(TENSOR_ORDER) if use[0] in CHAINS]
    assert len(uses) % NB == 0
    return {use: n % NB for n, use in enumerate(uses)}


BANK = chain_banks()


def chain_before(first, last):
    if first:
        held = {n: ("qk", 0, n) for n in range(NB)}
    else:
        held = {BANK[s, h, n]: (s, h - GH, n) for s, h, n in parse(TENSOR_ORDER) if s in CHAINS}
    before = {}
    for use in group_steps(TENSOR_ORDER, first, last):
        if use[0] in CHAINS:
            before[use] = held[BANK[use]]
            held[BANK[use]] = use
    return before, held


def tail_banks():
    _, held = chain_before(False, True)
    banks, before = {}, {}
    for k, use in enumerate(x for x in tail_steps(TENSOR_ORDER) if x[0] in CHAINS):
        banks[use], before[use] = k % NB, held[k % NB]
        held[k % NB] = use
    return banks, before


TAIL_BANK, TAIL_BEFORE = tail_banks()


def bank_of(step, j, n, tail):
    if tail and (step, j, n) in TAIL_BANK:
        return TAIL_BANK[step, j, n]
    return next((BANK[step, h, n] for h in (j, j + GH) if (step, h, n) in BANK), None)


def block_at(kt, i):
    return 7 * kt + i if kt < 4 else 13 + 3 * kt + i


ZERO_AT = 15
PLACES = block_at(7, 7) + 1


def sections(i):
    m = min(i, 3) + 1
    out = [(0, m, slice(block_at(0, i), block_at(m - 1, i) + 1, 7))]
    if i >= 4:
        out.append((4, i - 3, slice(block_at(4, i), block_at(i, i) + 1, 3)))
    return out


def build(nc, hidden, wq, wkv, wo, k0, s0, k1, s1, k2, s2, out):
    _, S, D = hidden.shape
    H = wo.shape[0] // DN
    DQ = wq.shape[1] // H
    SCALE = float(DQ) ** -0.5
    EPS = 1e-5
    NT = S // P
    NC = S // CH
    DC = D // P
    NG = H // GH
    assert (NT, NC, DC, D) == (8, 2, 4, CH) and NG >= 3
    NE = round(D * 0.8)
    UP = 2.0 ** 15
    INH = -4.0

    x_v = hidden.rearrange("b (t p) d -> p (b t) d", p=P)
    out_v = out.rearrange("b (t p) d -> p (b t) d", p=P)
    wq_v = wq.rearrange("(c p) (h e) -> p c h e", p=P, e=DQ)
    wk_v = wkv[:, 0:H * DN].rearrange("(c p) (h e) -> p c h e", p=P, e=DN)
    wv_v = wkv[:, H * DN:2 * H * DN].rearrange("(c p) (g e) -> p c g e", p=P, e=GH * DN)
    wo_v = wo.rearrange("(h p) d -> p h d", p=P)
    kern_v = [k.rearrange("(c p) n -> p c n", p=P) for k in (k0, k1, k2)]

    with ExitStack() as ctx:
        def sb(name, shape, dt):
            return ctx.enter_context(nc.sbuf_tensor(name, shape, dt))

        def psum(name, shape):
            return ctx.enter_context(nc.psum_tensor(name, shape, F32))

        def sem(name):
            return ctx.enter_context(nc.semaphore(name))

        xT = sb("xT", [P, 2, DC, S], F32R)
        res = sb("res", [P, NT, D], F32)
        v = sb("v", [P, 2, NT, GH * DN], F32R)
        pT = sb("pT", [P, 2, PLACES, P], F32R)
        p16 = sb("p16", [P, 2, 2 * S], F16)
        pt16 = sb("pt16", [P, 26, 2 * P], F16)
        qkT = sb("qkT", [P, 2, 2, 2, S], F32R)
        attn = sb("attn", [P, 2, S], F32R)
        probs = sb("probs", [P, 2, S], F32)
        raw = sb("raw", [P, 4, 512], F32)
        wqk = sb("wqk", [P, 2, 2, DC, DN], F32R)
        wvs = sb("wvs", [P, 2, DC, GH * DN], F32R)
        wos = sb("wos", [P, 2, D], F32R)
        ident = sb("ident", [P, P], F32)
        mask = sb("mask", [P, P], F32)
        one = sb("one", [P, 1], F32)
        negmax = sb("negmax", [P, NT], F32)
        rowsum = sb("rowsum", [P, 2, NT], F32)
        rinv = sb("rinv", [P, NT], F32)
        stats = sb("stats", [P, NT, 6], F32)
        mv = sb("mv", [P, NT, 2], F32)
        nrm = sb("nrm", [P, 5, 4], F32)
        slope = sb("slope", [P, DC], F32)
        base = sb("base", [P, DC], F32)
        scl = sb("scl", [P, 3], F32)
        scl2 = sb("scl2", [P, 3], F32)
        xn = probs[:, :, :].rearrange("p a (b d) -> p (a b) d", d=D)
        w_ffn = [wvs[:, :, :, :].rearrange("p w c e -> p (w c e)").rearrange("p (c n) -> p c n", n=D),
                 v[:, :, :, :].rearrange("p w t e -> p (w t e)")[:, 0:DC * D].rearrange("p (c n) -> p c n", n=D),
                 wqk[:, :, :, :, :].rearrange("p a b c e -> p (a b c e)").rearrange("p (c n) -> p c n", n=D)]
        h1T = qkT[:, :, :, :, :].rearrange("p a b c s -> p (a b c s)") \
            .rearrange("p (w c s) -> p w c s", w=2, c=DC)
        h2T = pT[:, :, :, :].rearrange("p w b s -> p (w b s)")[:, 0:2 * DC * S] \
            .rearrange("p (w c s) -> p w c s", w=2, c=DC)
        relu = probs[:, :, :].rearrange("p a (b s) -> p (a b) s", s=CH)

        psS = psum("psS", [P, 2, 1024])
        psC = psum("psC", [P, NB, CH])
        psT = psS[:, :, 0:CH]

        x_in = [sem(f"x_in{t}") for t in range(NT)]
        scl_in = sem("scl_in")
        loaded = {k: sem(f"loaded_{k}") for k in ("q", "k", "o", "v")}
        whi = {k: sem(f"whi_{k}") for k in ("q", "k", "o", "v")}
        wready = {k: sem(f"wready_{k}") for k in ("q", "k", "o", "v")}
        kern_in = sem("kern_in")
        w_ffn_ready = sem("w_ffn_ready")
        const_set = sem("const_set")
        const_ready = sem("const_ready")
        zero_ready = sem("zero_ready")
        done = {k: sem(f"{k}_done") for k in ("qk", "v", "s", "pv", "o")}
        hi_done = {k: sem(f"{k}_hi") for k in ("qk", "v", "pv")}
        lo_done = {k: sem(f"{k}_lo") for k in ("qk", "v", "pv")}
        exp_done = sem("exp_done")
        p_hi = sem("p_hi")
        p_lo = sem("p_lo")
        turned = [sem(f"turned{n}") for n in range(2)]
        turn_go = sem("turn_go")
        placed = sem("placed")
        masked = sem("masked")
        max_done = sem("max_done")
        rinv_done = sem("rinv_done")
        added = sem("added")
        evacuated = {"qk": lo_done["qk"], "v": lo_done["v"], "pv": lo_done["pv"], "o": added}
        ve_done = sem("ve_done")
        root_done = sem("root_done")
        xn_done = sem("xn_done")
        xt_done = sem("xt_done")
        xt_hi = sem("xt_hi")
        xt_lo = sem("xt_lo")
        chain_dve = sem("chain_dve")
        scl_ready = sem("scl_ready")
        f_done = sem("f_done")
        relu_done = sem("relu_done")
        h_hi = sem("h_hi")
        h_lo = sem("h_lo")
        y_done = sem("y_done")
        stored = sem("stored")
        block = ctx.enter_context(nc.Block())

        def count(g, j, per, n):
            return g * (GH * per) + (per * j + n)

        def turned_blocks(n):
            at = (0, 5, 11, 18)[n % 4]
            return pt16[:, at:at + n + 1, :].rearrange("p a (b s) -> p (a b) s", s=P)

        def wait(eng, s, value):
            if not isinstance(value, int) or value > 0:
                eng.wait_ge(s, value)

        def groups(eng, body):
            body(0, True, False)
            with eng.Fori(1, NG - 1) as g:
                body(g, False, False)
            body(NG - 1, False, True)

        @block.sync
        def _(sp):
            def load_head(kind, g, j):
                wait(sp, wready[kind], count(g, j, 1, 0))
                h = g * GH + j
                if kind == "o":
                    sp.dma_start(raw[:, 2, :], wo_v[:, bass.ds(h, 1), :].rearrange("p a d -> p (a d)")) \
                        .then_inc(loaded[kind], 16)
                else:
                    n, src = (0, wq_v) if kind == "q" else (1, wk_v)
                    sp.dma_start(raw[:, n, :].rearrange("p (c e) -> p c e", e=DN),
                                 src[:, :, bass.ds(h, 1), 0:DN].rearrange("p c a e -> p c (a e)")) \
                        .then_inc(loaded[kind], 16)

            def load_values(g, c):
                wait(sp, wready["v"], count(g, 0, 1, c))
                sp.dma_start(raw[:, 3, :].rearrange("p (c e) -> p c e", c=2),
                             wv_v[:, 2 * c:2 * c + 2, bass.ds(g, 1), :].rearrange("p c a e -> p c (a e)")) \
                    .then_inc(loaded["v"], 16)

            def load_kernel(layer):
                sp.dma_start(raw[:, 3, :].bitcast(U8).rearrange("p (c n) -> p c n", n=D), kern_v[layer]) \
                    .then_inc(kern_in, 16)

            for t in range(4):
                sp.dma_start(res[:, t, :], x_v[:, t, :]).then_inc(x_in[t], 16)
            load_head("q", 0, 0)
            load_head("k", 0, 0)
            for t in range(4, NT):
                sp.dma_start(res[:, t, :], x_v[:, t, :]).then_inc(x_in[t], 16)
            for n, s in enumerate((s0, s1, s2)):
                sp.dma_start(scl[:, n:n + 1], s.partition_broadcast(P)).then_inc(scl_in, 16)
            for c in range(GH):
                load_values(0, c)
            load_head("q", 0, 1)
            load_head("k", 0, 1)

            def load_slot(g, j, last):
                if not last:
                    load_head("q", g, j + 2)
                    load_head("k", g, j + 2)
                    load_values(g + 1, j)
                else:
                    sp.wait_ge(wready["v"], H)
                    if j == 1:
                        sp.wait_ge(w_ffn_ready, DC)
                    load_kernel(2 * j)
                load_head("o", g, j)

            def turn(g, steps, last):
                for step, j, n in steps:
                    if step == "l":
                        sp.wait_ge(p_lo, count(g, j, 8, n + 1))
                        sp.sem_inc(turn_go, 1)
                        sp.dma_start_transpose(turned_blocks(n), p16[:, n % 2, 0:2 * (n + 1) * P]) \
                            .then_inc(turned[n % 2], 16)
                        if n == 2:
                            load_slot(g, j, last)

            groups(sp, lambda g, first, last: turn(g, group_steps(VECTOR_ORDER, first, last), last))
            turn(NG - 1, tail_steps(VECTOR_ORDER), True)
            sp.wait_ge(w_ffn_ready, 2 * DC)
            load_kernel(1)
            for t in range(NT):
                sp.wait_ge(y_done, t + 1)
                sp.dma_start(out_v[:, t, :], res[:, t, :]).then_inc(stored, 16)
            sp.wait_ge(stored, 16 * NT)

        @block.gpsimd
        def _(pool):
            def cut(kind, n, count_ready, hi, lo):
                nc.gpsimd.tensor_tensor(hi, raw[:, n, :], one[:, :].to_broadcast([P, 512]), ALU.mult).then_inc(whi[kind], 1)
                pool.wait_ge(whi[kind], count_ready)
                nc.gpsimd.tensor_tensor(lo, raw[:, n, :], hi.bitcast(F32), ALU.subtract) \
                    .then_inc(wready[kind], 1)

            def cut_head(kind, g, j):
                pool.wait_ge(loaded[kind], count(g, j, 16, 16))
                if kind == "o":
                    wait(pool, done["o"], count(g, j, 8, 0))
                    cut("o", 2, count(g, j, 1, 1), wos[:, HI, :], wos[:, LO, :])
                else:
                    n = int(kind == "k")
                    wait(pool, done["qk"], count(g, j, 4, 2 * n - 2))
                    w = wqk[:, n].rearrange("p w c e -> p w (c e)")
                    cut(kind, n, count(g, j, 1, 1), w[:, HI], w[:, LO])

            def cut_values(g, c):
                pool.wait_ge(loaded["v"], count(g, 0, 16, 16 * c + 16))
                if c == 0:
                    wait(pool, done["v"], count(g, 0, PER_HEAD["v"], 0))
                w = wvs[:, :, 2 * c:2 * c + 2, :].rearrange("p w c e -> p w (c e)")
                cut("v", 3, count(g, 0, 1, c + 1), w[:, HI], w[:, LO])

            nc.gpsimd.memset(ident[:, :], 0.0).then_inc(const_set, 1)
            nc.gpsimd.memset(mask[:, :], 0.0).then_inc(const_set, 1)
            nc.gpsimd.memset(slope[:, :], 2.0).then_inc(const_set, 1)
            nc.gpsimd.memset(base[:, :], -1.0).then_inc(const_set, 1)
            nc.gpsimd.memset(one[:, :], 1.0).then_inc(const_set, 1)
            pool.wait_ge(const_set, 5)
            nc.gpsimd.affine_select(out=ident[:, :], in_=ident[:, :], compare_op=ALU.not_equal, fill=1.0,
                                    base=0, pattern=[[-1, P]], channel_multiplier=1).then_inc(const_ready, 1)
            nc.gpsimd.affine_select(out=mask[:, :], in_=mask[:, :], compare_op=ALU.is_ge, fill=-1e30,
                                    base=0, pattern=[[-1, P]], channel_multiplier=1).then_inc(const_ready, 1)
            for col, value in ((slope, 2.0), (base, -1.0)):
                part = col[:, NE // P:NE // P + 1]
                nc.gpsimd.affine_select(out=part, in_=part, compare_op=ALU.is_ge, fill=value * INH,
                                        base=NE % P - 1, pattern=[[0, 1]], channel_multiplier=-1) \
                    .then_inc(const_ready, 1)
            cut_head("q", 0, 0)
            cut_head("k", 0, 0)
            for c in range(GH):
                cut_values(0, c)
            cut_head("q", 0, 1)
            cut_head("k", 0, 1)

            def ffn_weights(n, nth):
                pool.wait_ge(kern_in, 16 * nth + 16)
                if n == 0:
                    pool.wait_ge(done["v"], NG * NT)
                    pool.wait_ge(const_ready, 4)
                elif n == 1:
                    pool.wait_ge(done["pv"], 2 * H)
                else:
                    pool.wait_ge(done["qk"], 4 * H)
                bits = raw[:, 3, :].bitcast(U8).rearrange("p (c n) -> p c n", n=D)
                for c in range(DC):
                    a, b = (2.0, -1.0) if n == 0 else (slope[:, c:c + 1], base[:, c:c + 1])
                    nc.gpsimd.tensor_scalar(w_ffn[n][:, c, :], bits[:, c, :], a, b, ALU.mult, ALU.add) \
                        .then_inc(w_ffn_ready, 1)

            def body(g, first, last):
                for j in range(GH):
                    if not last:
                        cut_head("q", g, j + 2)
                        cut_head("k", g, j + 2)
                        cut_values(g + 1, j)
                    else:
                        ffn_weights(2 * j, j)
                    cut_head("o", g, j)

            groups(pool, body)
            ffn_weights(1, 2)

        @block.scalar
        def _(act):
            def norm_root(b):
                act.wait_ge(ve_done, b + 1)
                nc.scalar.activation(nrm[:, 1, :], nrm[:, 0, :], ACT.Sqrt).then_inc(root_done, 1)

            def norm_hi(n):
                t = n % NT
                act.wait_ge(xt_done, n + 1)
                nc.scalar.activation(xT[:, HI, :, t * P:(t + 1) * P],
                                     psT[:, t % 2, :].rearrange("p (c s) -> p c s", s=P), ACT.Copy) \
                    .then_inc(xt_hi, 1)

            for b in range(NC):
                norm_root(b)
                for t in range(4 * b, 4 * b + 4):
                    norm_hi(t)

            def qk_hi(g, j, n, bank):
                side, c = n // 2, n % 2
                act.wait_ge(done["qk"], count(g, j, 4, n + 1))
                nc.scalar.activation(qkT[:, side, j % 2, HI, c * CH:(c + 1) * CH], psC[:, bank, :], ACT.Copy,
                                     scale=SCALE if side == 0 else 1.0).then_inc(hi_done["qk"], 1)

            for n in range(4):
                qk_hi(0, 0, n, n)

            def exponentials(g, j, n):
                width = (n + 1) * P
                off = P if n == 4 else 0
                act.wait_ge(max_done, count(g, j, 8, n + 1))
                wait(act, p_lo, count(g, j, 8, n - 1))
                nc.scalar.activation(probs[:, n % 2, 0:width], psS[:, n % 2, off:off + width], ACT.Exp,
                                     bias=negmax[:, n:n + 1], accum_out=rowsum[:, j % 2, n:n + 1]) \
                    .then_inc(exp_done, 1)

            def exp_hi(g, j, n):
                width = (n + 1) * P
                wait(act, turned[n % 2], count(g, j, 64, 16 * (n // 2)))
                act.wait_ge(exp_done, count(g, j, 8, n + 1))
                nc.scalar.activation(p16[:, n % 2, 0:width], probs[:, n % 2, 0:width], ACT.Copy, scale=UP) \
                    .then_inc(p_hi, 1)

            def place(g, j, n):
                act.wait_ge(turned[n % 2], count(g, j, 64, 16 * (n // 2) + 16))
                wait(act, done["pv"], count(g, j, 2, n // 4 - 1))
                src = turned_blocks(n).rearrange("p (w k) s -> p w k s", w=2)
                for first_kt, m, places in sections(n):
                    last = nc.scalar.activation(pT[:, :, places, :], src[:, :, first_kt:first_kt + m, :],
                                                ACT.Copy, scale=1.0 / UP)
                last.then_inc(placed, 1)

            def pv_hi(g, j, c, bank):
                act.wait_ge(done["pv"], count(g, j, 2, c + 1))
                wait(act, done["o"], count(g, j, 8, 4 * c - 4))
                nc.scalar.activation(attn[:, HI, c * CH:(c + 1) * CH], psC[:, bank, :], ACT.Copy) \
                    .then_inc(hi_done["pv"], 1)

            def scalar_steps(g, steps, tail=False):
                for step, j, n in steps:
                    bank = bank_of(step, j, n, tail)
                    if step == "e":
                        exponentials(g, j, n)
                    elif step == "h":
                        exp_hi(g, j, n)
                    elif step == "c":
                        place(g, j, n)
                    elif step == "qk":
                        qk_hi(g, j, n, bank)
                    elif step == "v":
                        act.wait_ge(done["v"], count(g, 0, PER_HEAD["v"], n + 1))
                        nc.scalar.activation(v[:, HI, n, :], psC[:, bank, 0:GH * DN], ACT.Copy) \
                            .then_inc(hi_done["v"], 1)
                    elif step == "pv":
                        pv_hi(g, j, n, bank)

            groups(act, lambda g, first, last: scalar_steps(g, group_steps(SCALAR_ORDER, first, last)))
            scalar_steps(NG - 1, tail_steps(SCALAR_ORDER), True)

            for b in range(NC):
                norm_root(NC + b)
                for t in range(4 * b, 4 * b + 4):
                    norm_hi(NT + t)

            act.wait_ge(scl_ready, 1)
            for layer, hT in enumerate((h1T, h2T)):
                for n in range(NT):
                    c, do = n // 4, n % 4
                    m = NT * layer + n
                    act.wait_ge(f_done, m + 1)
                    if m >= 4:
                        act.wait_ge(h_lo, m - 3)
                    nc.scalar.activation(relu[:, n % 4, :], psC[:, n % 4, :], ACT.Relu,
                                         scale=scl2[:, layer:layer + 1]).then_inc(relu_done, 1)
                    nc.scalar.activation(hT[:, HI, do, c * CH:(c + 1) * CH], psC[:, n % 4, :], ACT.Relu,
                                         scale=scl2[:, layer:layer + 1]).then_inc(h_hi, 1)

        @block.vector
        def _(dve):
            links = [0]

            def link(ins):
                links[0] += 1
                ins.then_inc(chain_dve, 1)
                dve.wait_ge(chain_dve, links[0])

            def norm_batch(b, round_):
                for t in range(4 * b, 4 * b + 4):
                    if round_ == 0:
                        dve.wait_ge(x_in[t], 16)
                    else:
                        dve.wait_ge(added, NT * (H - 1) + t + 1)
                    link(nc.vector.bn_stats(stats[:, t, :], res[:, t, :]))
                    link(nc.vector.bn_aggr(mv[:, t, :], stats[:, t, :]))
                ve, root, inv, a, bb = (nrm[:, k, :] for k in range(5))
                nc.vector.tensor_scalar_add(ve, mv[:, 4 * b:4 * b + 4, 1], EPS).then_inc(ve_done, 1)
                dve.wait_ge(root_done, NC * round_ + b + 1)
                link(nc.vector.reciprocal(inv, root))
                link(nc.vector.tensor_tensor(a, inv, inv, ALU.mult))
                link(nc.vector.tensor_tensor(bb, a, ve, ALU.mult))
                link(nc.vector.tensor_scalar(a, bb, -0.5, 1.5, ALU.mult, ALU.add))
                link(nc.vector.tensor_tensor(bb, inv, a, ALU.mult))
                for t in range(4 * b, 4 * b + 4):
                    n = NT * round_ + t
                    if t >= 4:
                        dve.wait_ge(xt_done, n - 3)
                    nc.vector.tensor_scalar(xn[:, t % 4, :], res[:, t, :], mv[:, t, 0:1], bb[:, t % 4:t % 4 + 1],
                                            ALU.subtract, ALU.mult).then_inc(xn_done, 1)
                for t in range(4 * b, 4 * b + 4):
                    n = NT * round_ + t
                    dve.wait_ge(xt_hi, n + 1)
                    nc.vector.tensor_tensor(xT[:, LO, :, t * P:(t + 1) * P],
                                            psT[:, t % 2, :].rearrange("p (c s) -> p c s", s=P),
                                            xT[:, HI, :, t * P:(t + 1) * P].bitcast(F32), ALU.subtract) \
                        .then_inc(xt_lo, 1)

            nc.vector.memset(pT[:, :, ZERO_AT, :].bitcast(F32), 0.0).then_inc(zero_ready, 1)
            for b in range(NC):
                norm_batch(b, 0)

            def qk_lo(g, j, n, bank):
                side, c = n // 2, n % 2
                hi, lo = (qkT[:, side, j % 2, w, c * CH:(c + 1) * CH] for w in (HI, LO))
                dve.wait_ge(hi_done["qk"], count(g, j, 4, n + 1))
                nc.vector.scalar_tensor_tensor(lo, psC[:, bank, :], SCALE if side == 0 else 1.0, hi.bitcast(F32),
                                               ALU.mult, ALU.subtract).then_inc(lo_done["qk"], 1)

            def pv_lo(g, j, c, bank):
                hi, lo = (attn[:, w, c * CH:(c + 1) * CH] for w in (HI, LO))
                dve.wait_ge(hi_done["pv"], count(g, j, 2, c + 1))
                nc.vector.tensor_tensor(lo, psC[:, bank, :], hi.bitcast(F32), ALU.subtract) \
                    .then_inc(lo_done["pv"], 1)

            def invert_sums(g, j):
                dve.wait_ge(exp_done, count(g, j, 8, 8))
                wait(dve, added, count(g, j, 8, 0))
                nc.vector.reciprocal(rinv[:, :], rowsum[:, j % 2, :]).then_inc(rinv_done, 1)

            def add_output(g, j, t, bank):
                if t == 0:
                    dve.wait_ge(rinv_done, count(g, j, 1, 1))
                dve.wait_ge(done["o"], count(g, j, 8, t + 1))
                wait(dve, added, count(g, j, 8, t - 7))
                nc.vector.scalar_tensor_tensor(res[:, t, :], psC[:, bank, :], rinv[:, t:t + 1], res[:, t, :],
                                               ALU.mult, ALU.add).then_inc(added, 1)

            for n in range(4):
                qk_lo(0, 0, n, n)

            def vector_steps(g, steps, tail=False):
                for step, j, n in steps:
                    bank = bank_of(step, j, n, tail)
                    width = (n + 1) * P
                    if step == "m":
                        off = P if n == 4 else 0
                        diag = psS[:, n % 2, off + width - P:off + width]
                        dve.wait_ge(done["s"], count(g, j, 8, n + 1))
                        nc.vector.tensor_tensor(diag, diag, mask[:, :], ALU.add).then_inc(masked, 1)
                        dve.wait_ge(masked, count(g, j, 8, n + 1))
                        nc.vector.tensor_reduce(negmax[:, n:n + 1], psS[:, n % 2, off:off + width], AX_X, ALU.max,
                                                negate=True).then_inc(max_done, 1)
                    elif step == "l":
                        dve.wait_ge(p_hi, count(g, j, 8, n + 1))
                        nc.vector.scalar_tensor_tensor(p16[:, n % 2, width:2 * width], probs[:, n % 2, 0:width], UP,
                                                       p16[:, n % 2, 0:width], ALU.mult, ALU.subtract) \
                            .then_inc(p_lo, 1)
                    elif step == "qk":
                        qk_lo(g, j, n, bank)
                    elif step == "v":
                        dve.wait_ge(hi_done["v"], count(g, 0, PER_HEAD["v"], n + 1))
                        nc.vector.tensor_tensor(v[:, LO, n, :], psC[:, bank, 0:GH * DN], v[:, HI, n, :].bitcast(F32),
                                                ALU.subtract).then_inc(lo_done["v"], 1)
                    elif step == "pv":
                        pv_lo(g, j, n, bank)
                    elif step == "o":
                        if n == 0:
                            invert_sums(g, j)
                        add_output(g, j, n, bank)

            dve.wait_ge(const_ready, 2)
            groups(dve, lambda g, first, last: vector_steps(g, group_steps(VECTOR_ORDER, first, last)))
            vector_steps(NG - 1, tail_steps(VECTOR_ORDER), True)

            dve.wait_ge(scl_in, 48)
            nc.vector.tensor_scalar_mul(scl2[:, :], scl[:, :], 2.0).then_inc(scl_ready, 1)
            for b in range(NC):
                norm_batch(b, 1)
            for layer, hT in enumerate((h1T, h2T)):
                for n in range(NT):
                    c, do = n // 4, n % 4
                    m = NT * layer + n
                    dve.wait_ge(relu_done, m + 1)
                    dve.wait_ge(h_hi, m + 1)
                    nc.vector.tensor_tensor(hT[:, LO, do, c * CH:(c + 1) * CH], relu[:, n % 4, :],
                                            hT[:, HI, do, c * CH:(c + 1) * CH].bitcast(F32), ALU.subtract) \
                        .then_inc(h_lo, 1)
            for t in range(NT):
                dve.wait_ge(f_done, 2 * NT + t + 1)
                nc.vector.scalar_tensor_tensor(res[:, t, :], psC[:, t % 4, :], scl[:, 2:3], res[:, t, :],
                                               ALU.mult, ALU.add).then_inc(y_done, 1)

        @block.tensor
        def _(pe):
            def chain(out_ap, terms):
                for k, (w, x) in enumerate(terms):
                    last = nc.tensor.matmul(out_ap, w, x, start=(k == 0), stop=(k == len(terms) - 1))
                return last

            def halves(w, x):
                return [(w(HI), x(HI)), (w(HI), x(LO)), (w(LO), x(HI))]

            def norm_transpose(n):
                t = n % NT
                pe.wait_ge(xn_done, n + 1)
                if t >= 2:
                    pe.wait_ge(xt_lo, n - 1)
                for c in range(DC):
                    last = nc.tensor.transpose(psT[:, t % 2, c * P:(c + 1) * P],
                                               xn[:, t % 4, c * P:(c + 1) * P], ident[:, :])
                last.then_inc(xt_done, 1)

            def project_qk(g, j, n, bank):
                side, c = n // 2, n % 2
                if c == 0:
                    pe.wait_ge(wready["qk"[side]], count(g, j, 1, 1))
                terms = []
                for d in range(DC):
                    terms += halves(lambda w: wqk[:, side, w, d, :], lambda w: xT[:, w, d, c * CH:(c + 1) * CH])
                chain(psC[:, bank, :], terms).then_inc(done["qk"], 1)

            pe.wait_ge(const_ready, 1)
            for t in range(NT):
                norm_transpose(t)
            for n in range(4):
                pe.wait_ge(xt_lo, 4 if n % 2 == 0 else NT)
                project_qk(0, 0, n, n)

            def values(g, j, c, bank):
                pe.wait_ge(placed, count(g, j, 8, 4 * c + 4))
                if c == 0 and j == 0:
                    pe.wait_ge(lo_done["v"], count(g, 0, PER_HEAD["v"], NT))
                keys = 4 * c + 4
                for kt in range(keys):
                    i = max(4 * c, kt)
                    at, n = block_at(kt, i), 4 * c + 4 - i
                    cols = slice(ZERO_AT, at + 1, at - ZERO_AT) if n == 1 else slice(at, at + n)
                    o = psC[:, bank, (4 - max(n, 2)) * P:]
                    if n == 1:
                        o = o.rearrange("p (b s) -> p b s", s=P)
                    terms = halves(lambda w: v[:, w, kt, j % GH * DN:(j % GH + 1) * DN],
                                   lambda w: pT[:, w, cols, :] if n == 1 else
                                   pT[:, w, cols, :].rearrange("p b s -> p (b s)"))
                    for k, (a, b) in enumerate(terms):
                        last = nc.tensor.matmul(o, a, b, start=(kt == 0 and k == 0),
                                                stop=(kt == keys - 1 and k == 2))
                last.then_inc(done["pv"], 1)

            def project_out(g, j, t, bank):
                if t == 0:
                    pe.wait_ge(wready["o"], count(g, j, 1, 1))
                if t % 4 == 0:
                    pe.wait_ge(lo_done["pv"], count(g, j, 2, t // 4 + 1))
                chain(psC[:, bank, :], halves(lambda w: attn[:, w, t * P:(t + 1) * P], lambda w: wos[:, w, :])) \
                    .then_inc(done["o"], 1)

            def bank_free(g, before):
                kind, j, n = before
                pe.wait_ge(evacuated[kind], count(g, j, PER_HEAD[kind], n + 1))

            def scores(g, j, n):
                if n == 0:
                    pe.wait_ge(lo_done["qk"], count(g, j, 4, 4))
                wait(pe, exp_done, count(g, j, 8, n - 1))
                off = P if n == 4 else 0
                spans = {4: [(0, 3 * P), (3 * P, 5 * P)]}.get(n, [(0, min(4, max(2, n + 1)) * P)])
                if n > 4:
                    spans.append((CH, (n + 1) * P))
                for a, b in spans:
                    last = chain(psS[:, n % 2, off + a:off + b],
                                 halves(lambda w: qkT[:, 0, j % 2, w, n * P:(n + 1) * P],
                                        lambda w: qkT[:, 1, j % 2, w, a:b]))
                last.then_inc(done["s"], 1)

            def project_v(g, n, bank):
                if n == 0:
                    pe.wait_ge(wready["v"], count(g, 0, 1, GH))
                terms = []
                for d in range(DC):
                    terms += halves(lambda w: xT[:, w, d, n * P:(n + 1) * P], lambda w: wvs[:, w, d, :])
                chain(psC[:, bank, 0:GH * DN], terms).then_inc(done["v"], 1)

            def tensor_steps(g, steps, before, tail=False):
                for step, j, n in steps:
                    bank = bank_of(step, j, n, tail)
                    if step in CHAINS:
                        bank_free(g, before[step, j, n])
                    if step == "s":
                        scores(g, j, n)
                    elif step == "qk":
                        project_qk(g, j, n, bank)
                    elif step == "v":
                        project_v(g, n, bank)
                    elif step == "pv":
                        values(g, j, n, bank)
                    elif step == "o":
                        project_out(g, j, n, bank)

            pe.wait_ge(zero_ready, 1)
            groups(pe, lambda g, first, last: tensor_steps(g, group_steps(TENSOR_ORDER, first, last),
                                                           chain_before(first, last)[0]))
            tensor_steps(NG - 1, tail_steps(TENSOR_ORDER), TAIL_BEFORE, True)

            for t in range(NT):
                norm_transpose(NT + t)
            for layer, src in enumerate((xT, h1T)):
                for n in range(NT):
                    c, do = n // 4, n % 4
                    m = NT * layer + n
                    if do == 0:
                        if layer == 0:
                            pe.wait_ge(xt_lo, NT + 4 * c + 4)
                        else:
                            pe.wait_ge(h_lo, 4 * c + 4)
                    if n == 0:
                        pe.wait_ge(w_ffn_ready, (DC, 3 * DC)[layer])
                    if layer == 0 and n == 0:
                        pe.wait_ge(added, NT * H)
                    if m >= 4:
                        pe.wait_ge(h_lo, m - 3)
                    terms = [(w_ffn[layer][:, d, do * P:(do + 1) * P], src[:, w, d, c * CH:(c + 1) * CH])
                             for d in range(DC) for w in (HI, LO)]
                    chain(psC[:, n % 4, :], terms).then_inc(f_done, 1)
            for t in range(NT):
                if t == 0:
                    pe.wait_ge(w_ffn_ready, 3 * DC)
                if t < 4:
                    pe.wait_ge(h_lo, 2 * NT - 3 + t)
                    pe.wait_ge(h_lo, NT + 4)
                else:
                    pe.wait_ge(y_done, t - 3)
                if t == 4:
                    pe.wait_ge(h_lo, 2 * NT)
                terms = [(h2T[:, w, d, t * P:(t + 1) * P], w_ffn[2][:, d, :]) for d in range(DC) for w in (HI, LO)]
                chain(psC[:, t % 4, :], terms).then_inc(f_done, 1)


_INS = ["L0_attn_hidden_states", "L0_attn_wq", "L0_attn_wkv", "L0_attn_wo", "L0_ffn_k0", "L0_ffn_s0",
        "L0_ffn_k1", "L0_ffn_s1", "L0_ffn_k2", "L0_ffn_s2"]


def kernel(**inputs):
    import numpy as _np
    import concourse.bacc as _bacc
    from concourse import mybir as _mybir
    from concourse.bass_utils import run_bass_kernel_spmd as _run

    nc = _bacc.Bacc("TRN2", target_bir_lowering=False, num_devices=1)
    arrays, args = {}, []
    for name in _INS:
        a = _np.ascontiguousarray(inputs[name])
        arrays[f"in_{name}"] = a
        args.append(nc.dram_tensor(f"in_{name}", a.shape, _mybir.dt.from_np(a.dtype), kind="ExternalInput").ap())
    shape = inputs["L0_attn_hidden_states"].shape
    args.append(nc.dram_tensor("out", shape, _mybir.dt.float32, kind="ExternalOutput").ap())
    build(nc, *args)
    r = _run(nc, [arrays], core_ids=[0])
    return r.results[0]["out"]
```

```python
from contextlib import ExitStack

import concourse.bass as bass
from concourse import mybir

ALU = mybir.AluOpType
ACT = mybir.ActivationFunctionType
AX_X = mybir.AxisListType.X
F32 = mybir.dt.float32
F32R = mybir.dt.float32r
F16 = mybir.dt.float16
U8 = mybir.dt.uint8

P = 128
CH = 512
DN = 128
GH = 2
HI, LO = 0, 1

TENSOR_ORDER = """
    qk0@1 s0@0 qk1@1 s1@0 o0@-1 qk2@1 s2@0 o1@-1 s3@0 o2@-1 qk3@1 s4@0 o3@-1 pv1@-1 s5@0 v0@0 v1@0
    s6@0 v2@0 v3@0 s7@0 o4@-1 v4@0 v5@0 s0@1 o5@-1 qk0@2 v6@0 s1@1 v7@0 qk1@2 s2@1 s3@1 o6@-1 o7@-1
    pv0@0 s4@1 qk2@2 o0@0 s5@1 o1@0 pv1@0 o2@0 s6@1 o3@0 qk3@2 o4@0 s7@1 o5@0 pv0@1 o6@0 o7@0"""
SCALAR_ORDER = """
    qk0@1 e0@0 c5@-1 qk1@1 e1@0 h0@0 c6@-1 qk2@1 e2@0 h1@0 c7@-1 h2@0 qk3@1 e3@0 h3@0 c0@0 e4@0
    pv1@-1 c1@0 v0@0 h4@0 e5@0 v1@0 h5@0 c2@0 v2@0 c3@0 e6@0 v3@0 h6@0 c4@0 v4@0 e7@0 v5@0 h7@0 e0@1
    c5@0 h0@1 qk0@2 v6@0 v7@0 e1@1 c6@0 qk1@2 e2@1 h1@1 h2@1 pv0@0 e3@1 c7@0 c0@1 c1@1 h3@1 qk2@2
    c2@1 e4@1 h4@1 e5@1 pv1@0 c3@1 h5@1 qk3@2 e6@1 h6@1 pv0@1 c4@1 e7@1 h7@1"""
VECTOR_ORDER = """
    m0@0 l7@-1 m1@0 qk0@1 o0@-1 l0@0 qk1@1 m2@0 qk2@1 l1@0 o1@-1 o2@-1 m3@0 l2@0 m4@0 o3@-1 l3@0
    qk3@1 m5@0 pv1@-1 v0@0 l4@0 m6@0 v1@0 l5@0 v2@0 m7@0 v3@0 o4@-1 l6@0 v4@0 m0@1 v5@0 o5@-1 l7@0
    m1@1 qk0@2 l0@1 v6@0 v7@0 m2@1 m3@1 qk1@2 l1@1 l2@1 pv0@0 o6@-1 o7@-1 m4@1 o0@0 m5@1 l3@1 qk2@2
    o1@0 l4@1 o2@0 pv1@0 o3@0 m6@1 l5@1 qk3@2 o4@0 o5@0 m7@1 l6@1 pv0@1 o6@0 o7@0"""
FIRST_QK = (0, 2, 1, 3)
TENSOR_END = """
    o2@0 s6@1 s7@1 o3@0 o4@0 o5@0 pv0@1 o6@0 o7@0"""
SCALAR_END = """
    h5@1 e6@1 h6@1 c4@1 e7@1 h7@1 pv0@1"""
VECTOR_END = """
    pv1@0 m6@1 m7@1 l5@1 o3@0 l6@1 o4@0 o5@0 l7@1 pv0@1 o6@0 o7@0"""
FIRST_STEPS = ([("root", 0)] + [("turn", t) for t in range(4)] + [("root", 1), ("qk", 0)]
               + [("turn", t) for t in range(4, 8)] + [("qk", k) for k in range(1, 4)])
ENDS = {TENSOR_ORDER: TENSOR_END, SCALAR_ORDER: SCALAR_END, VECTOR_ORDER: VECTOR_END}
FFN_CHAINS = ([(0, n) for n in range(4)] + [(1, n) for n in range(4)] + [(0, n) for n in range(4, 8)]
              + [(2, 0), (2, 1)] + [(1, n) for n in range(4, 8)] + [(2, n) for n in range(2, 8)])
HIDDEN = [x for x in FFN_CHAINS if x[0] < 2]
CHAINS = ("qk", "v", "pv", "o")
NB = 4
PER_HEAD = {"qk": 4, "v": 8 // GH, "pv": 2, "o": 8}


def parse(order):
    out = []
    for word in order.split():
        name, head = word.split("@")
        out.append((name[:-1], int(head), int(name[-1])))
    return out


def group_steps(order, first, last):
    steps = [x for x in parse(order) if not (first and x[1] < 0) and not (last and x[1] >= GH)]
    end = parse(ENDS.get(order, "")) if last else []
    return steps[:min(steps.index(x) for x in end if x in steps)] + end if end else steps


def tail_steps(order):
    left = [(step, h + GH, n) for step, h, n in parse(order) if h < 0]
    left = [x for x in left if x not in parse(ENDS.get(order, ""))]
    ends = [x for x in left if x[0] == "o" and x[2] >= 4]
    outs = [x for x in left if x[0] == "o" and x[2] < 4]
    return [x for x in left if x[0] != "o"][:-1] + outs + [("pv", GH - 1, 1)], ends


def chain_banks():
    uses = [use for use in parse(TENSOR_ORDER) if use[0] in CHAINS]
    assert len(uses) % NB == 0
    return {use: n % NB for n, use in enumerate(uses)}


BANK = chain_banks()


def chain_before(first, last):
    if first:
        held = {k: ("qk", 0, k) for k in range(NB)}
    else:
        held = {BANK[s, h, n]: (s, h - GH, n) for s, h, n in parse(TENSOR_ORDER) if s in CHAINS}
    before = {}
    for use in group_steps(TENSOR_ORDER, first, last):
        if use[0] in CHAINS:
            before[use] = held[BANK[use]]
            held[BANK[use]] = use
    return before, held


def tail_banks():
    _, held = chain_before(False, True)
    banks, before = {}, {}
    for k, use in enumerate(sum(tail_steps(TENSOR_ORDER), [])):
        banks[use], before[use] = k % NB, held[k % NB]
        held[k % NB] = use
    return banks, before


TAIL_BANK, TAIL_BEFORE = tail_banks()


def ffn_bank(use):
    return (TAIL_BANK["o", GH - 1, 4] + FFN_CHAINS.index(use)) % NB


def bank_of(step, j, n, tail):
    if tail and (step, j, n) in TAIL_BANK:
        return TAIL_BANK[step, j, n]
    return next((BANK[step, h, n] for h in (j, j + GH) if (step, h, n) in BANK), None)


def block_at(kt, i):
    return 7 * kt + i if kt < 4 else 13 + 3 * kt + i


ZERO_AT = 15
PLACES = block_at(7, 7) + 1


def sections(i):
    m = min(i, 3) + 1
    out = [(0, m, slice(block_at(0, i), block_at(m - 1, i) + 1, 7))]
    if i >= 4:
        out.append((4, i - 3, slice(block_at(4, i), block_at(i, i) + 1, 3)))
    return out


def build(nc, hidden, wq, wkv, wo, k0, s0, k1, s1, k2, s2, out):
    _, S, D = hidden.shape
    H = wo.shape[0] // DN
    DQ = wq.shape[1] // H
    SCALE = float(DQ) ** -0.5
    EPS = 1e-5
    NT = S // P
    NC = S // CH
    DC = D // P
    NG = H // GH
    assert (NT, NC, DC, D) == (8, 2, 4, CH) and NG >= 3
    NE = round(D * 0.8)
    UP = 2.0 ** 15
    INH = -4.0

    x_v = hidden.rearrange("b (t p) d -> p (b t) d", p=P)
    out_v = out.rearrange("b (t p) d -> p (b t) d", p=P)
    wq_v = wq.rearrange("(c p) (h e) -> p c h e", p=P, e=DQ)
    wk_v = wkv[:, 0:H * DN].rearrange("(c p) (h e) -> p c h e", p=P, e=DN)
    wv_v = wkv[:, H * DN:2 * H * DN].rearrange("(c p) (g e) -> p c g e", p=P, e=GH * DN)
    wo_v = wo.rearrange("(h p) d -> p h d", p=P)
    kern_v = [k.rearrange("(c p) n -> p c n", p=P) for k in (k0, k1, k2)]

    with ExitStack() as ctx:
        def sb(name, shape, dt):
            return ctx.enter_context(nc.sbuf_tensor(name, shape, dt))

        def psum(name, shape):
            return ctx.enter_context(nc.psum_tensor(name, shape, F32))

        def sem(name):
            return ctx.enter_context(nc.semaphore(name))

        xT = sb("xT", [P, 2, DC, S], F32R)
        res = sb("res", [P, NT, D], F32)
        v = sb("v", [P, 2, NT, GH * DN], F32R)
        pT = sb("pT", [P, 2, PLACES, P], F32R)
        p16 = sb("p16", [P, 2, 2 * S], F16)
        pt16 = sb("pt16", [P, 26, 2 * P], F16)
        qkT = sb("qkT", [P, 2, 2, 2, S], F32R)
        attn = sb("attn", [P, 2, S], F32R)
        probs = sb("probs", [P, 2, S], F32)
        raw = sb("raw", [P, 4, 512], F32)
        wqk = sb("wqk", [P, 2, 2, DC, DN], F32R)
        wvs = sb("wvs", [P, 2, DC, GH * DN], F32R)
        wos = sb("wos", [P, 2, D], F32R)
        ident = sb("ident", [P, P], F32)
        mask = sb("mask", [P, P], F32)
        one = sb("one", [P, 1], F32)
        negmax = sb("negmax", [P, NT], F32)
        rowsum = sb("rowsum", [P, 2, NT], F32)
        rinv = sb("rinv", [P, NT], F32)
        stats = sb("stats", [P, NT, 6], F32)
        mv = sb("mv", [P, NT, 2], F32)
        nrm = sb("nrm", [P, 5, 4], F32)
        slope = sb("slope", [P, DC], F32)
        base = sb("base", [P, DC], F32)
        scl = sb("scl", [P, 3], F32)
        scl2 = sb("scl2", [P, 3], F32)
        xn = probs[:, :, :].rearrange("p a (b d) -> p (a b) d", d=D)
        w_ffn = [wvs[:, :, :, :].rearrange("p w c e -> p (w c e)").rearrange("p (c n) -> p c n", n=D),
                 v[:, :, :, :].rearrange("p w t e -> p (w t e)")[:, 0:DC * D].rearrange("p (c n) -> p c n", n=D),
                 wqk[:, :, :, :, :].rearrange("p a b c e -> p (a b c e)").rearrange("p (c n) -> p c n", n=D)]
        h1T = qkT[:, :, :, :, :].rearrange("p a b c s -> p (a b c s)") \
            .rearrange("p (w c s) -> p w c s", w=2, c=DC)
        h2T = pT[:, :, :, :].rearrange("p w b s -> p (w b s)")[:, 0:2 * DC * S] \
            .rearrange("p (w c s) -> p w c s", w=2, c=DC)
        relu = p16[:, :, :].rearrange("p a s -> p (a s)").bitcast(F32).rearrange("p (b s) -> p b s", s=CH)

        psS = psum("psS", [P, 2, 1024])
        psC = psum("psC", [P, NB, CH])
        psT = psS[:, :, :].rearrange("p a (b s) -> p (a b) s", s=CH)

        x_in = [sem(f"x_in{t}") for t in range(NT)]
        scl_in = sem("scl_in")
        loaded = {k: sem(f"loaded_{k}") for k in ("q", "k", "o", "v")}
        whi = {k: sem(f"whi_{k}") for k in ("q", "k", "o", "v")}
        wready = {k: sem(f"wready_{k}") for k in ("q", "k", "o", "v")}
        kern_in = sem("kern_in")
        w_ffn_ready = sem("w_ffn_ready")
        const_set = sem("const_set")
        const_ready = sem("const_ready")
        zero_ready = sem("zero_ready")
        done = {k: sem(f"{k}_done") for k in ("qk", "v", "s", "pv", "o")}
        hi_done = {k: sem(f"{k}_hi") for k in ("qk", "v", "pv")}
        lo_done = {k: sem(f"{k}_lo") for k in ("qk", "v", "pv")}
        exp_done = sem("exp_done")
        p_hi = sem("p_hi")
        p_lo = sem("p_lo")
        turned = [sem(f"turned{n}") for n in range(2)]
        turn_go = sem("turn_go")
        placed = sem("placed")
        masked = sem("masked")
        max_done = sem("max_done")
        rinv_done = sem("rinv_done")
        added = sem("added")
        evacuated = {"qk": lo_done["qk"], "v": lo_done["v"], "pv": lo_done["pv"], "o": added}
        stats_done = sem("stats_done")
        mv_done = sem("mv_done")
        ve_done = sem("ve_done")
        root_done = sem("root_done")
        xn_done = sem("xn_done")
        xt_done = sem("xt_done")
        xt_hi = sem("xt_hi")
        xt_lo = sem("xt_lo")
        chain_dve = sem("chain_dve")
        scl_ready = sem("scl_ready")
        f_done = sem("f_done")
        relu_done = sem("relu_done")
        h_hi = sem("h_hi")
        h_lo = sem("h_lo")
        y_done = sem("y_done")
        stored = sem("stored")
        block = ctx.enter_context(nc.Block())

        def count(g, j, per, n):
            return g * (GH * per) + (per * j + n)

        def turned_blocks(n):
            at = (0, 5, 11, 18)[n % 4]
            return pt16[:, at:at + n + 1, :].rearrange("p a (b s) -> p (a b) s", s=P)

        def wait(eng, s, value):
            if not isinstance(value, int) or value > 0:
                eng.wait_ge(s, value)

        def groups(eng, body):
            body(0, True, False)
            with eng.Fori(1, NG - 1) as g:
                body(g, False, False)
            body(NG - 1, False, True)

        @block.sync
        def _(sp):
            def load_head(kind, g, j):
                wait(sp, wready[kind], count(g, j, 1, 0))
                h = g * GH + j
                if kind == "o":
                    sp.dma_start(raw[:, 2, :], wo_v[:, bass.ds(h, 1), :].rearrange("p a d -> p (a d)")) \
                        .then_inc(loaded[kind], 16)
                else:
                    n, src = (0, wq_v) if kind == "q" else (1, wk_v)
                    sp.dma_start(raw[:, n, :].rearrange("p (c e) -> p c e", e=DN),
                                 src[:, :, bass.ds(h, 1), 0:DN].rearrange("p c a e -> p c (a e)")) \
                        .then_inc(loaded[kind], 16)

            def load_values(g, c):
                wait(sp, wready["v"], count(g, 0, 1, c))
                sp.dma_start(raw[:, 3, :].rearrange("p (c e) -> p c e", c=2),
                             wv_v[:, 2 * c:2 * c + 2, bass.ds(g, 1), :].rearrange("p c a e -> p c (a e)")) \
                    .then_inc(loaded["v"], 16)

            def load_kernel(layer):
                sp.dma_start(raw[:, 3, :].bitcast(U8).rearrange("p (c n) -> p c n", n=D), kern_v[layer]) \
                    .then_inc(kern_in, 16)

            for t in range(4):
                sp.dma_start(res[:, t, :], x_v[:, t, :]).then_inc(x_in[t], 16)
            load_head("q", 0, 0)
            load_head("k", 0, 0)
            for t in range(4, NT):
                sp.dma_start(res[:, t, :], x_v[:, t, :]).then_inc(x_in[t], 16)
            for n, s in enumerate((s0, s1, s2)):
                sp.dma_start(scl[:, n:n + 1], s.partition_broadcast(P)).then_inc(scl_in, 16)
            for c in range(GH):
                load_values(0, c)
            load_head("q", 0, 1)
            load_head("k", 0, 1)

            def load_slot(g, j, last):
                if not last:
                    load_head("q", g, j + 2)
                    load_head("k", g, j + 2)
                    load_values(g + 1, j)
                else:
                    sp.wait_ge(wready["v"], H)
                    if j == 1:
                        sp.wait_ge(w_ffn_ready, DC)
                    load_kernel(2 * j)
                load_head("o", g, j)

            def turn(g, steps, last):
                for step, j, n in steps:
                    if step == "l":
                        sp.wait_ge(p_lo, count(g, j, 8, n + 1))
                        sp.sem_inc(turn_go, 1)
                        sp.dma_start_transpose(turned_blocks(n), p16[:, n % 2, 0:2 * (n + 1) * P]) \
                            .then_inc(turned[n % 2], 16)
                        if n == 2:
                            load_slot(g, j, last)

            groups(sp, lambda g, first, last: turn(g, group_steps(VECTOR_ORDER, first, last), last))
            turn(NG - 1, tail_steps(VECTOR_ORDER)[0], True)
            sp.wait_ge(w_ffn_ready, 2 * DC)
            load_kernel(1)
            for t in range(NT):
                sp.wait_ge(y_done, t + 1)
                sp.dma_start(out_v[:, t, :], res[:, t, :]).then_inc(stored, 16)
            sp.wait_ge(stored, 16 * NT)

        @block.gpsimd
        def _(pool):
            def cut(kind, n, count_ready, hi, lo):
                nc.gpsimd.tensor_tensor(hi, raw[:, n, :], one[:, :].to_broadcast([P, 512]), ALU.mult) \
                    .then_inc(whi[kind], 1)
                pool.wait_ge(whi[kind], count_ready)
                nc.gpsimd.tensor_tensor(lo, raw[:, n, :], hi.bitcast(F32), ALU.subtract) \
                    .then_inc(wready[kind], 1)

            def cut_head(kind, g, j):
                pool.wait_ge(loaded[kind], count(g, j, 16, 16))
                if kind == "o":
                    wait(pool, done["o"], count(g, j, 8, 0))
                    cut("o", 2, count(g, j, 1, 1), wos[:, HI, :], wos[:, LO, :])
                else:
                    n = int(kind == "k")
                    early = kind == "q" and j == 1 and isinstance(g, int) and g == 0
                    wait(pool, done["qk"], 3 if early else count(g, j, 4, 2 * n - 2))
                    w = wqk[:, n].rearrange("p w c e -> p w (c e)")
                    cut(kind, n, count(g, j, 1, 1), w[:, HI], w[:, LO])

            def cut_values(g, c):
                pool.wait_ge(loaded["v"], count(g, 0, 16, 16 * c + 16))
                if c == 0:
                    wait(pool, done["v"], count(g, 0, PER_HEAD["v"], 0))
                w = wvs[:, :, 2 * c:2 * c + 2, :].rearrange("p w c e -> p w (c e)")
                cut("v", 3, count(g, 0, 1, c + 1), w[:, HI], w[:, LO])

            nc.gpsimd.memset(ident[:, :], 0.0).then_inc(const_set, 1)
            nc.gpsimd.memset(mask[:, :], 0.0).then_inc(const_set, 1)
            nc.gpsimd.memset(slope[:, :], 2.0).then_inc(const_set, 1)
            nc.gpsimd.memset(base[:, :], -1.0).then_inc(const_set, 1)
            nc.gpsimd.memset(one[:, :], 1.0).then_inc(const_set, 1)
            pool.wait_ge(const_set, 5)
            nc.gpsimd.affine_select(out=ident[:, :], in_=ident[:, :], compare_op=ALU.not_equal, fill=1.0,
                                    base=0, pattern=[[-1, P]], channel_multiplier=1).then_inc(const_ready, 1)
            nc.gpsimd.affine_select(out=mask[:, :], in_=mask[:, :], compare_op=ALU.is_ge, fill=-1e30,
                                    base=0, pattern=[[-1, P]], channel_multiplier=1).then_inc(const_ready, 1)
            for col, value in ((slope, 2.0), (base, -1.0)):
                part = col[:, NE // P:NE // P + 1]
                nc.gpsimd.affine_select(out=part, in_=part, compare_op=ALU.is_ge, fill=value * INH,
                                        base=NE % P - 1, pattern=[[0, 1]], channel_multiplier=-1) \
                    .then_inc(const_ready, 1)
            cut_head("q", 0, 0)
            cut_head("k", 0, 0)
            for c in range(GH):
                cut_values(0, c)
            cut_head("q", 0, 1)
            cut_head("k", 0, 1)

            def ffn_weights(n, nth):
                pool.wait_ge(kern_in, 16 * nth + 16)
                if n == 0:
                    pool.wait_ge(done["v"], NG * NT)
                    pool.wait_ge(const_ready, 4)
                elif n == 1:
                    pool.wait_ge(done["pv"], 2 * H)
                else:
                    pool.wait_ge(done["qk"], 4 * H)
                bits = raw[:, 3, :].bitcast(U8).rearrange("p (c n) -> p c n", n=D)
                for c in range(DC):
                    a, b = (2.0, -1.0) if n == 0 else (slope[:, c:c + 1], base[:, c:c + 1])
                    nc.gpsimd.tensor_scalar(w_ffn[n][:, c, :], bits[:, c, :], a, b, ALU.mult, ALU.add) \
                        .then_inc(w_ffn_ready, 1)

            def body(g, first, last):
                for j in range(GH):
                    if not last:
                        cut_head("q", g, j + 2)
                        cut_head("k", g, j + 2)
                        cut_values(g + 1, j)
                    else:
                        ffn_weights(2 * j, j)
                    cut_head("o", g, j)

            groups(pool, body)
            ffn_weights(1, 2)

        @block.scalar
        def _(act):
            def norm_root(b):
                act.wait_ge(ve_done, b + 1)
                nc.scalar.activation(nrm[:, 1, :], nrm[:, 0, :], ACT.Sqrt).then_inc(root_done, 1)

            def norm_hi(n):
                t = n % NT
                act.wait_ge(xt_done, n + 1)
                nc.scalar.activation(xT[:, HI, :, t * P:(t + 1) * P],
                                     psT[:, t % 4, :].rearrange("p (c s) -> p c s", s=P), ACT.Copy) \
                    .then_inc(xt_hi, 1)

            def qk_hi(g, j, n, bank, nth=None):
                side, c = n // 2, n % 2
                act.wait_ge(done["qk"], count(g, j, 4, (n if nth is None else nth) + 1))
                nc.scalar.activation(qkT[:, side, j % 2, HI, c * CH:(c + 1) * CH], psC[:, bank, :], ACT.Copy,
                                     scale=SCALE if side == 0 else 1.0).then_inc(hi_done["qk"], 1)


            for step, n in FIRST_STEPS:
                if step == "root":
                    norm_root(n)
                elif step == "turn":
                    norm_hi(n)
                elif step == "qk":
                    qk_hi(0, 0, FIRST_QK[n], n, n)

            def exponentials(g, j, n):
                width = (n + 1) * P
                off = P if n == 4 else 0
                act.wait_ge(max_done, count(g, j, 8, n + 1))
                wait(act, p_lo, count(g, j, 8, n - 1))
                nc.scalar.activation(probs[:, n % 2, 0:width], psS[:, n % 2, off:off + width], ACT.Exp,
                                     bias=negmax[:, n:n + 1], accum_out=rowsum[:, j % 2, n:n + 1]) \
                    .then_inc(exp_done, 1)

            def exp_hi(g, j, n):
                width = (n + 1) * P
                wait(act, turned[n % 2], count(g, j, 64, 16 * (n // 2)))
                act.wait_ge(exp_done, count(g, j, 8, n + 1))
                nc.scalar.activation(p16[:, n % 2, 0:width], probs[:, n % 2, 0:width], ACT.Copy, scale=UP) \
                    .then_inc(p_hi, 1)

            def place(g, j, n):
                act.wait_ge(turned[n % 2], count(g, j, 64, 16 * (n // 2) + 16))
                wait(act, done["pv"], count(g, j, 2, n // 4 - 1))
                src = turned_blocks(n).rearrange("p (w k) s -> p w k s", w=2)
                for first_kt, m, places in sections(n):
                    last = nc.scalar.activation(pT[:, :, places, :], src[:, :, first_kt:first_kt + m, :],
                                                ACT.Copy, scale=1.0 / UP)
                last.then_inc(placed, 1)

            def pv_hi(g, j, c, bank):
                act.wait_ge(done["pv"], count(g, j, 2, c + 1))
                wait(act, done["o"], count(g, j, 8, 4 * c - 4))
                nc.scalar.activation(attn[:, HI, c * CH:(c + 1) * CH], psC[:, bank, :], ACT.Copy) \
                    .then_inc(hi_done["pv"], 1)

            def scalar_steps(g, steps, tail=False):
                for step, j, n in steps:
                    bank = bank_of(step, j, n, tail)
                    if step == "e":
                        exponentials(g, j, n)
                    elif step == "h":
                        exp_hi(g, j, n)
                    elif step == "c":
                        place(g, j, n)
                    elif step == "qk":
                        qk_hi(g, j, n, bank)
                    elif step == "v":
                        act.wait_ge(done["v"], count(g, 0, PER_HEAD["v"], n + 1))
                        nc.scalar.activation(v[:, HI, n, :], psC[:, bank, 0:GH * DN], ACT.Copy) \
                            .then_inc(hi_done["v"], 1)
                    elif step == "pv":
                        pv_hi(g, j, n, bank)

            groups(act, lambda g, first, last: scalar_steps(g, group_steps(SCALAR_ORDER, first, last)))
            scalar_steps(NG - 1, tail_steps(SCALAR_ORDER)[0][:-1], True)

            def ffn_hi(m):
                layer, n = HIDDEN[m]
                c, do, bank = n // 4, n % 4, ffn_bank((layer, n))
                act.wait_ge(f_done, FFN_CHAINS.index((layer, n)) + 1)
                if m >= 4:
                    act.wait_ge(h_lo, m - 3)
                nc.scalar.activation(relu[:, m % 4, :], psC[:, bank, :], ACT.Relu,
                                     scale=scl2[:, layer:layer + 1]).then_inc(relu_done, 1)
                nc.scalar.activation((h1T, h2T)[layer][:, HI, do, c * CH:(c + 1) * CH], psC[:, bank, :],
                                     ACT.Relu, scale=scl2[:, layer:layer + 1]).then_inc(h_hi, 1)

            norm_root(2)
            scalar_steps(NG - 1, tail_steps(SCALAR_ORDER)[0][-1:], True)
            for t in range(4):
                norm_hi(NT + t)
            act.wait_ge(scl_ready, 1)
            ffn_hi(0)
            ffn_hi(1)
            norm_root(3)
            for m in range(2, 4):
                ffn_hi(m)
            for t in range(4, NT):
                norm_hi(NT + t)
            for m in range(4, 2 * NT):
                ffn_hi(m)

        @block.vector
        def _(dve):
            links = [0]

            def link(ins):
                links[0] += 1
                ins.then_inc(chain_dve, 1)
                dve.wait_ge(chain_dve, links[0])

            def norm_stats(n):
                t = n % NT
                if n < NT:
                    dve.wait_ge(x_in[t], 16)
                else:
                    dve.wait_ge(added, NT * (H - 1) + t + 1)
                nc.vector.bn_stats(stats[:, t, :], res[:, t, :]).then_inc(stats_done, 1)

            def norm_scale(b):
                first = 4 * (b % NC)
                for t in range(first, first + 4):
                    dve.wait_ge(stats_done, 4 * b + t - first + 1)
                    nc.vector.bn_aggr(mv[:, t, :], stats[:, t, :]).then_inc(mv_done, 1)
                dve.wait_ge(mv_done, 4 * b + 4)
                ve, root, inv, a, bb = (nrm[:, k, :] for k in range(5))
                nc.vector.tensor_scalar_add(ve, mv[:, first:first + 4, 1], EPS).then_inc(ve_done, 1)
                dve.wait_ge(root_done, b + 1)
                link(nc.vector.reciprocal(inv, root))
                link(nc.vector.tensor_tensor(a, inv, inv, ALU.mult))
                link(nc.vector.tensor_tensor(bb, a, ve, ALU.mult))
                link(nc.vector.tensor_scalar(a, bb, -0.5, 1.5, ALU.mult, ALU.add))
                link(nc.vector.tensor_tensor(bb, inv, a, ALU.mult))

            def norm_apply(n):
                t = n % NT
                if t >= 4:
                    dve.wait_ge(xt_done, n - 3)
                nc.vector.tensor_scalar(xn[:, t % 4, :], res[:, t, :], mv[:, t, 0:1], nrm[:, 4, t % 4:t % 4 + 1],
                                        ALU.subtract, ALU.mult).then_inc(xn_done, 1)

            def norm_lo(n):
                t = n % NT
                dve.wait_ge(xt_hi, n + 1)
                nc.vector.tensor_tensor(xT[:, LO, :, t * P:(t + 1) * P],
                                        psT[:, t % 4, :].rearrange("p (c s) -> p c s", s=P),
                                        xT[:, HI, :, t * P:(t + 1) * P].bitcast(F32), ALU.subtract) \
                    .then_inc(xt_lo, 1)

            def qk_lo(g, j, n, bank, nth=None):
                side, c = n // 2, n % 2
                hi, lo = (qkT[:, side, j % 2, w, c * CH:(c + 1) * CH] for w in (HI, LO))
                dve.wait_ge(hi_done["qk"], count(g, j, 4, (n if nth is None else nth) + 1))
                nc.vector.scalar_tensor_tensor(lo, psC[:, bank, :], SCALE if side == 0 else 1.0, hi.bitcast(F32),
                                               ALU.mult, ALU.subtract).then_inc(lo_done["qk"], 1)

            def pv_lo(g, j, c, bank):
                hi, lo = (attn[:, w, c * CH:(c + 1) * CH] for w in (HI, LO))
                dve.wait_ge(hi_done["pv"], count(g, j, 2, c + 1))
                nc.vector.tensor_tensor(lo, psC[:, bank, :], hi.bitcast(F32), ALU.subtract) \
                    .then_inc(lo_done["pv"], 1)

            def invert_sums(g, j):
                dve.wait_ge(exp_done, count(g, j, 8, 8))
                wait(dve, added, count(g, j, 8, 0))
                nc.vector.reciprocal(rinv[:, :], rowsum[:, j % 2, :]).then_inc(rinv_done, 1)

            def add_output(g, j, t, bank):
                if t == 0:
                    dve.wait_ge(rinv_done, count(g, j, 1, 1))
                dve.wait_ge(done["o"], count(g, j, 8, t + 1))
                wait(dve, added, count(g, j, 8, t - 7))
                nc.vector.scalar_tensor_tensor(res[:, t, :], psC[:, bank, :], rinv[:, t:t + 1], res[:, t, :],
                                               ALU.mult, ALU.add).then_inc(added, 1)

            nc.vector.memset(pT[:, :, ZERO_AT, :].bitcast(F32), 0.0).then_inc(zero_ready, 1)
            for t in range(4):
                norm_stats(t)
            norm_scale(0)
            for t in range(4):
                norm_apply(t)
            norm_stats(4)
            norm_lo(0)
            norm_lo(1)
            norm_stats(5)
            norm_lo(2)
            norm_lo(3)
            norm_stats(6)
            norm_stats(7)
            norm_scale(1)
            for t in range(4, NT):
                norm_apply(t)
            for step, n in FIRST_STEPS[FIRST_STEPS.index(("turn", 3)) + 1:]:
                if step == "turn":
                    norm_lo(n)
                elif step == "qk":
                    qk_lo(0, 0, FIRST_QK[n], n, n)

            def vector_steps(g, steps, tail=False):
                for step, j, n in steps:
                    bank = bank_of(step, j, n, tail)
                    width = (n + 1) * P
                    if step == "m":
                        off = P if n == 4 else 0
                        diag = psS[:, n % 2, off + width - P:off + width]
                        dve.wait_ge(done["s"], count(g, j, 8, n + 1))
                        nc.vector.tensor_tensor(diag, diag, mask[:, :], ALU.add).then_inc(masked, 1)
                        dve.wait_ge(masked, count(g, j, 8, n + 1))
                        nc.vector.tensor_reduce(negmax[:, n:n + 1], psS[:, n % 2, off:off + width], AX_X, ALU.max,
                                                negate=True).then_inc(max_done, 1)
                    elif step == "l":
                        dve.wait_ge(p_hi, count(g, j, 8, n + 1))
                        nc.vector.scalar_tensor_tensor(p16[:, n % 2, width:2 * width], probs[:, n % 2, 0:width], UP,
                                                       p16[:, n % 2, 0:width], ALU.mult, ALU.subtract) \
                            .then_inc(p_lo, 1)
                    elif step == "qk":
                        qk_lo(g, j, n, bank)
                    elif step == "v":
                        dve.wait_ge(hi_done["v"], count(g, 0, PER_HEAD["v"], n + 1))
                        nc.vector.tensor_tensor(v[:, LO, n, :], psC[:, bank, 0:GH * DN], v[:, HI, n, :].bitcast(F32),
                                                ALU.subtract).then_inc(lo_done["v"], 1)
                    elif step == "pv":
                        pv_lo(g, j, n, bank)
                    elif step == "o":
                        if n == 0:
                            invert_sums(g, j)
                        add_output(g, j, n, bank)

            dve.wait_ge(const_ready, 2)
            groups(dve, lambda g, first, last: vector_steps(g, group_steps(VECTOR_ORDER, first, last)))

            def ffn_lo(m):
                layer, n = HIDDEN[m]
                c, do = n // 4, n % 4
                hT = (h1T, h2T)[layer]
                dve.wait_ge(relu_done, m + 1)
                dve.wait_ge(h_hi, m + 1)
                nc.vector.tensor_tensor(hT[:, LO, do, c * CH:(c + 1) * CH], relu[:, m % 4, :],
                                        hT[:, HI, do, c * CH:(c + 1) * CH].bitcast(F32), ALU.subtract) \
                    .then_inc(h_lo, 1)

            dve.wait_ge(scl_in, 48)
            nc.vector.tensor_scalar_mul(scl2[:, :], scl[:, :], 2.0).then_inc(scl_ready, 1)
            early, late = tail_steps(VECTOR_ORDER)
            for step in early[:-1]:
                vector_steps(NG - 1, [step], True)
                if step[0] == "o":
                    norm_stats(NT + step[2])
            norm_scale(2)
            for t in range(4):
                norm_apply(NT + t)
            vector_steps(NG - 1, early[-1:], True)
            for t in range(4):
                norm_lo(NT + t)
            for step in late:
                vector_steps(NG - 1, [step], True)
                norm_stats(NT + step[2])
            norm_scale(3)
            ffn_lo(0)
            norm_apply(NT + 4)
            ffn_lo(1)
            norm_apply(NT + 5)
            norm_apply(NT + 6)
            ffn_lo(2)
            norm_apply(NT + 7)
            ffn_lo(3)
            for t in range(4, NT):
                norm_lo(NT + t)
            for k in range(4, len(FFN_CHAINS)):
                layer, t = FFN_CHAINS[k]
                if layer < 2:
                    ffn_lo(HIDDEN.index((layer, t)))
                else:
                    dve.wait_ge(f_done, k + 1)
                    nc.vector.scalar_tensor_tensor(res[:, t, :], psC[:, ffn_bank((2, t)), :], scl[:, 2:3],
                                                   res[:, t, :], ALU.mult, ALU.add).then_inc(y_done, 1)

        @block.tensor
        def _(pe):
            def chain(out_ap, terms):
                for k, (w, x) in enumerate(terms):
                    last = nc.tensor.matmul(out_ap, w, x, start=(k == 0), stop=(k == len(terms) - 1))
                return last

            def halves(w, x):
                return [(w(HI), x(HI)), (w(HI), x(LO)), (w(LO), x(HI))]

            def norm_transpose(n):
                t = n % NT
                pe.wait_ge(xn_done, n + 1)
                if t >= 4:
                    pe.wait_ge(xt_lo, n - 3)
                for c in range(DC):
                    last = nc.tensor.transpose(psT[:, t % 4, c * P:(c + 1) * P],
                                               xn[:, t % 4, c * P:(c + 1) * P], ident[:, :])
                last.then_inc(xt_done, 1)

            def project_qk(g, j, n, bank):
                side, c = n // 2, n % 2
                if c == 0:
                    pe.wait_ge(wready["qk"[side]], count(g, j, 1, 1))
                terms = []
                for d in range(DC):
                    terms += halves(lambda w: wqk[:, side, w, d, :], lambda w: xT[:, w, d, c * CH:(c + 1) * CH])
                chain(psC[:, bank, :], terms).then_inc(done["qk"], 1)

            pe.wait_ge(const_ready, 1)
            for step, n in FIRST_STEPS:
                if step == "turn":
                    norm_transpose(n)
                elif step == "qk":
                    pe.wait_ge(xt_lo, 4 * (FIRST_QK[n] % 2) + 4)
                    project_qk(0, 0, FIRST_QK[n], n)

            def values(g, j, c, bank):
                pe.wait_ge(placed, count(g, j, 8, 4 * c + 4))
                if c == 0 and j == 0:
                    pe.wait_ge(lo_done["v"], count(g, 0, PER_HEAD["v"], NT))
                keys = 4 * c + 4
                for kt in range(keys):
                    i = max(4 * c, kt)
                    at, n = block_at(kt, i), 4 * c + 4 - i
                    cols = slice(ZERO_AT, at + 1, at - ZERO_AT) if n == 1 else slice(at, at + n)
                    o = psC[:, bank, (4 - max(n, 2)) * P:]
                    if n == 1:
                        o = o.rearrange("p (b s) -> p b s", s=P)
                    terms = halves(lambda w: v[:, w, kt, j % GH * DN:(j % GH + 1) * DN],
                                   lambda w: pT[:, w, cols, :] if n == 1 else
                                   pT[:, w, cols, :].rearrange("p b s -> p (b s)"))
                    for k, (a, b) in enumerate(terms):
                        last = nc.tensor.matmul(o, a, b, start=(kt == 0 and k == 0),
                                                stop=(kt == keys - 1 and k == 2))
                last.then_inc(done["pv"], 1)

            def project_out(g, j, t, bank):
                if t == 0:
                    pe.wait_ge(wready["o"], count(g, j, 1, 1))
                if t % 4 == 0:
                    pe.wait_ge(lo_done["pv"], count(g, j, 2, t // 4 + 1))
                chain(psC[:, bank, :], halves(lambda w: attn[:, w, t * P:(t + 1) * P], lambda w: wos[:, w, :])) \
                    .then_inc(done["o"], 1)

            def bank_free(g, before):
                kind, j, n = before
                pe.wait_ge(evacuated[kind], count(g, j, PER_HEAD[kind], n + 1))

            def scores(g, j, n):
                if j == 0 and isinstance(g, int) and g == 0:
                    if n % 4 == 0:
                        pe.wait_ge(lo_done["qk"], n // 2 + 2)
                elif n == 0:
                    pe.wait_ge(lo_done["qk"], count(g, j, 4, 4))
                wait(pe, exp_done, count(g, j, 8, n - 1))
                off = P if n == 4 else 0
                spans = {4: [(0, 3 * P), (3 * P, 5 * P)]}.get(n, [(0, min(4, max(2, n + 1)) * P)])
                if n > 4:
                    spans.append((CH, (n + 1) * P))
                for a, b in spans:
                    last = chain(psS[:, n % 2, off + a:off + b],
                                 halves(lambda w: qkT[:, 0, j % 2, w, n * P:(n + 1) * P],
                                        lambda w: qkT[:, 1, j % 2, w, a:b]))
                last.then_inc(done["s"], 1)

            def project_v(g, n, bank):
                if n == 0:
                    pe.wait_ge(wready["v"], count(g, 0, 1, GH))
                terms = []
                for d in range(DC):
                    terms += halves(lambda w: xT[:, w, d, n * P:(n + 1) * P], lambda w: wvs[:, w, d, :])
                chain(psC[:, bank, 0:GH * DN], terms).then_inc(done["v"], 1)

            def tensor_steps(g, steps, before, tail=False):
                for step, j, n in steps:
                    bank = bank_of(step, j, n, tail)
                    if step in CHAINS:
                        bank_free(g, before[step, j, n])
                    if step == "s":
                        scores(g, j, n)
                    elif step == "qk":
                        project_qk(g, j, n, bank)
                    elif step == "v":
                        project_v(g, n, bank)
                    elif step == "pv":
                        values(g, j, n, bank)
                    elif step == "o":
                        project_out(g, j, n, bank)

            pe.wait_ge(zero_ready, 1)
            groups(pe, lambda g, first, last: tensor_steps(g, group_steps(TENSOR_ORDER, first, last),
                                                           chain_before(first, last)[0]))

            def hidden_done(layer, c):
                return HIDDEN.index((layer, 4 * c + 3)) + 1

            def ffn_chain(k):
                layer, n = FFN_CHAINS[k]
                c, do = n // 4, n % 4
                if do == 0 and layer == 0:
                    pe.wait_ge(xt_lo, NT + 4 * c + 4)
                elif do == 0:
                    pe.wait_ge(h_lo, hidden_done(layer - 1, c))
                if n == 0:
                    pe.wait_ge(w_ffn_ready, DC if layer == 0 else 3 * DC)
                if k < 4:
                    pe.wait_ge(added, NT * H - 3 + k)
                else:
                    before = FFN_CHAINS[:k - 3]
                    if before[-1][0] < 2:
                        pe.wait_ge(h_lo, sum(x[0] < 2 for x in before))
                    else:
                        pe.wait_ge(y_done, sum(x[0] == 2 for x in before))
                if layer < 2:
                    src = (xT, h1T)[layer]
                    terms = [(w_ffn[layer][:, d, do * P:(do + 1) * P], src[:, w, d, c * CH:(c + 1) * CH])
                             for d in range(DC) for w in (HI, LO)]
                else:
                    terms = [(h2T[:, w, d, n * P:(n + 1) * P], w_ffn[2][:, d, :])
                             for d in range(DC) for w in (HI, LO)]
                chain(psC[:, ffn_bank((layer, n)), :], terms).then_inc(f_done, 1)

            early, late = tail_steps(TENSOR_ORDER)
            tensor_steps(NG - 1, early, TAIL_BEFORE, True)
            for t in range(4):
                norm_transpose(NT + t)
            tensor_steps(NG - 1, late, TAIL_BEFORE, True)
            for k in range(4):
                ffn_chain(k)
            for t in range(4, NT):
                norm_transpose(NT + t)
            for k in range(4, len(FFN_CHAINS)):
                ffn_chain(k)


_INS = ["L0_attn_hidden_states", "L0_attn_wq", "L0_attn_wkv", "L0_attn_wo", "L0_ffn_k0", "L0_ffn_s0",
        "L0_ffn_k1", "L0_ffn_s1", "L0_ffn_k2", "L0_ffn_s2"]


def kernel(**inputs):
    import numpy as _np
    import concourse.bacc as _bacc
    from concourse import mybir as _mybir
    from concourse.bass_utils import run_bass_kernel_spmd as _run

    nc = _bacc.Bacc("TRN2", target_bir_lowering=False, num_devices=1)
    arrays, args = {}, []
    for name in _INS:
        a = _np.ascontiguousarray(inputs[name])
        arrays[f"in_{name}"] = a
        args.append(nc.dram_tensor(f"in_{name}", a.shape, _mybir.dt.from_np(a.dtype), kind="ExternalInput").ap())
    shape = inputs["L0_attn_hidden_states"].shape
    args.append(nc.dram_tensor("out", shape, _mybir.dt.float32, kind="ExternalOutput").ap())
    build(nc, *args)
    r = _run(nc, [arrays], core_ids=[0])
    return r.results[0]["out"]
```
